# Optimizing a Trainium2 kernel written in Bass

```python
import numpy as np
import jax
import jax.numpy as jnp

def _softmax(x, axis=-1):
    return jax.nn.softmax(x, axis=axis)

def _gelu(x):
    return jax.nn.gelu(x, approximate=True)

def _silu(x):
    return jax.nn.silu(x)

def _sigmoid(x):
    return jax.nn.sigmoid(x)

def _layernorm(x, axis=-1, eps=1e-05):
    m = jnp.mean(x, axis=axis, keepdims=True)
    v = jnp.var(x, axis=axis, keepdims=True)
    return (x - m) / jnp.sqrt(v + eps)

def _scatter_add(tgt, idx, src, axis=0):
    return tgt.at[idx].add(src)

def _segment_sum(src, seg, n):
    return jax.ops.segment_sum(src, seg, n)
kernel_name = 'mk_flamingo_gated_d1_seqx_r8_9eaa69'

def setup_inputs(seed: int=0):
    np.random.seed(seed)
    _w = jnp.asarray

    def _rec_inputs():
        import jax
        import jax.numpy as jnp
        _rk = jax.random.key(seed)
        x = -0.0005207 + 1.001 * jax.random.normal(jax.random.fold_in(_rk, 1), (64, 64, 256), jnp.float32)
        _lenS = 64 - jax.random.randint(jax.random.fold_in(_rk, 7), (64,), 0, max(1, 64 // 4) + 1, jnp.int32)
        _lenS2 = 64 - jax.random.randint(jax.random.fold_in(_rk, 8), (64,), 0, max(1, 64 // 4) + 1, jnp.int32)
        _ctx_2048P = jax.random.normal(jax.random.fold_in(_rk, 11), (64, 16, 256), jnp.float32)
        _ctx_2048c = jax.random.dirichlet(jax.random.fold_in(_rk, 511), 0.3 * jnp.ones((16,), jnp.float32), (64, 64))
        _ctx_2048t = jnp.einsum('bsk,bkd->bsd', _ctx_2048c, _ctx_2048P)
        _ctx_2048t = _ctx_2048t * jax.lax.rsqrt(jnp.mean(jnp.square(_ctx_2048t)) + 1e-12) * 0.953939
        ctx_2048 = -0.000514642 + 1.00011 * (_ctx_2048t + 0.3 * jax.random.normal(jax.random.fold_in(_rk, 611), (64, 64, 256), jnp.float32))
        _g = jax.random.normal(jax.random.fold_in(_rk, 9001), (2, 1), jnp.float32)
        _g = jnp.sign(_g) * jnp.maximum(jnp.abs(_g), 1.0) + (_g == 0) * 1.0
        g_xattn = _g[0]
        g_ffn = _g[1]
        return (x, ctx_2048, g_xattn, g_ffn)
    x, ctx_2048, g_xattn, g_ffn = _rec_inputs()

    def _L0_xattn_setup():
        import jax, jax.numpy as jnp
        import numpy as np
        from math import sqrt
        key = jax.random.key(seed)
        kq, kk, kv = jax.random.split(key, 3)
        B, D, N = (8, 128, 256)
        Q = jax.random.normal(kq, (B, D, N), dtype=jnp.float32)
        K = jax.random.normal(kk, (B, D, N), dtype=jnp.float32)
        V = jax.random.normal(kv, (B, D, N), dtype=jnp.float32)
        return {'Q': Q, 'K': K, 'V': V}
    _L0_xattn_all = _L0_xattn_setup()
    _L0_xattn_in = {k: v for k, v in _L0_xattn_all.items() if k in ()}
    del _L0_xattn_all

    def _L0_ffn_setup():
        import jax, jax.numpy as jnp
        import numpy as np
        E = 32
        G = 8
        TKG = 4
        K = 4
        D = 256
        H = 128
        HS = 512
        SCALE = 2.5
        CAP = 128

        def relu2(x):
            r = jnp.maximum(x, 0.0)
            return r * r

        def route_tokens(scores, bias_corr):
            T = scores.shape[0]
            scores_c = scores + bias_corr
            group_scores = jax.lax.top_k(scores_c.reshape(T, G, E // G), 2)[0].sum(-1)
            _, group_idx = jax.lax.top_k(group_scores, TKG)
            group_mask = jnp.zeros((T, G), scores.dtype).at[jnp.arange(T)[:, None], group_idx].set(1.0)
            score_mask = jnp.repeat(group_mask, E // G, axis=1)
            masked = jnp.where(score_mask > 0, scores_c, 0.0)
            _, topk_idx = jax.lax.top_k(masked, K)
            topk_w = jnp.take_along_axis(scores, topk_idx, axis=1)
            topk_w = topk_w / (topk_w.sum(-1, keepdims=True) + 1e-20)
            return (topk_idx, topk_w * SCALE)
        key = jax.random.key(seed)
        ks = jax.random.split(key, 6)
        B, S = (2, 256)
        return dict(hidden_states=jax.random.normal(ks[0], (B, S, D), jnp.float32), gate_w=jax.random.normal(ks[1], (E, D), jnp.float32) * 0.02, bias_corr=jnp.zeros((E,), jnp.float32), up_w=jax.random.normal(ks[2], (E, H, D), jnp.float32) * 0.02, down_w=jax.random.normal(ks[3], (E, D, H), jnp.float32) * 0.02, shared_up_w=jax.random.normal(ks[4], (HS, D), jnp.float32) * 0.02, shared_down_w=jax.random.normal(ks[5], (D, HS), jnp.float32) * 0.02)
    _L0_ffn_all = _L0_ffn_setup()
    _L0_ffn_in = {k: v for k, v in _L0_ffn_all.items() if k in ('gate_w', 'bias_corr', 'up_w', 'down_w', 'shared_up_w', 'shared_down_w')}
    del _L0_ffn_all
    return {'x': x, 'ctx_2048': ctx_2048, 'g_xattn': g_xattn, 'g_ffn': g_ffn, 'L0_ffn_gate_w': _L0_ffn_in['gate_w'], 'L0_ffn_bias_corr': _L0_ffn_in['bias_corr'], 'L0_ffn_up_w': _L0_ffn_in['up_w'], 'L0_ffn_down_w': _L0_ffn_in['down_w'], 'L0_ffn_shared_up_w': _L0_ffn_in['shared_up_w'], 'L0_ffn_shared_down_w': _L0_ffn_in['shared_down_w']}

def reference(x, ctx_2048, g_xattn, g_ffn, L0_ffn_gate_w, L0_ffn_bias_corr, L0_ffn_up_w, L0_ffn_down_w, L0_ffn_shared_up_w, L0_ffn_shared_down_w):
    import jax
    import jax.numpy as jnp

    def _L0_xattn_ref(Q, K, V):
        import jax, jax.numpy as jnp
        import numpy as np
        from math import sqrt
        dk = Q.shape[1]
        x = jnp.einsum('bdn,bdm->bnm', Q, K) / sqrt(dk)
        score = jax.nn.sigmoid(x)
        out = jnp.einsum('bvn,bnm->bvm', V, score)
        return out

    def _L0_ffn_ref(hidden_states, gate_w, bias_corr, up_w, down_w, shared_up_w, shared_down_w):
        import jax, jax.numpy as jnp
        import numpy as np
        E = 32
        G = 8
        TKG = 4
        K = 4
        D = 256
        H = 128
        HS = 512
        SCALE = 2.5
        CAP = 128

        def relu2(x):
            r = jnp.maximum(x, 0.0)
            return r * r

        def route_tokens(scores, bias_corr):
            T = scores.shape[0]
            scores_c = scores + bias_corr
            group_scores = jax.lax.top_k(scores_c.reshape(T, G, E // G), 2)[0].sum(-1)
            _, group_idx = jax.lax.top_k(group_scores, TKG)
            group_mask = jnp.zeros((T, G), scores.dtype).at[jnp.arange(T)[:, None], group_idx].set(1.0)
            score_mask = jnp.repeat(group_mask, E // G, axis=1)
            masked = jnp.where(score_mask > 0, scores_c, 0.0)
            _, topk_idx = jax.lax.top_k(masked, K)
            topk_w = jnp.take_along_axis(scores, topk_idx, axis=1)
            topk_w = topk_w / (topk_w.sum(-1, keepdims=True) + 1e-20)
            return (topk_idx, topk_w * SCALE)
        B, S, _ = hidden_states.shape
        T = B * S
        flat = hidden_states.reshape(T, D)
        logits = flat @ gate_w.T
        scores = jax.nn.sigmoid(logits)
        topk_idx, topk_w = route_tokens(scores, bias_corr)
        e_flat = topk_idx.reshape(-1)
        oh = jax.nn.one_hot(e_flat, E, dtype=jnp.int32)
        pos = jnp.take_along_axis(jnp.cumsum(oh, axis=0) - 1, e_flat[:, None], axis=1)[:, 0]
        tok = jnp.repeat(jnp.arange(T), K)
        valid = pos < CAP
        xe = jnp.zeros((E, CAP, D), flat.dtype).at[e_flat, pos].set(flat[tok], mode='drop')
        h = relu2(jnp.einsum('ecd,ehd->ech', xe, up_w))
        ye = jnp.einsum('ech,edh->ecd', h, down_w)
        gathered = ye[e_flat, jnp.minimum(pos, CAP - 1)]
        gathered = jnp.where(valid[:, None], gathered, 0.0) * topk_w.reshape(-1)[:, None]
        routed = gathered.reshape(T, K, D).sum(axis=1).reshape(B, S, D)
        shared = relu2(hidden_states @ shared_up_w.T) @ shared_down_w.T
        return routed + shared
    x = x + jnp.tanh(g_xattn[0]) * _L0_xattn_ref(_layernorm(x, axis=-1), ctx_2048, ctx_2048)
    x = x + jnp.tanh(g_ffn[0]) * _L0_ffn_ref(_layernorm(x, axis=-1), L0_ffn_gate_w, L0_ffn_bias_corr, L0_ffn_up_w, L0_ffn_down_w, L0_ffn_shared_up_w, L0_ffn_shared_down_w)
    return x

_drawn_inputs = setup_inputs


def setup_inputs(seed=0):
    import zlib

    import numpy as np

    out = dict(_drawn_inputs(seed))
    spreads = {'L0_ffn_bias_corr': (0.0, 0.8)}
    factors = {'L0_ffn_gate_w': 8.0,
     'L0_ffn_up_w': 8.0,
     'L0_ffn_down_w': 8.0,
     'L0_ffn_shared_up_w': 7.506,
     'L0_ffn_shared_down_w': 6.851}
    for name, (base, spread) in spreads.items():
        noise = np.random.default_rng([zlib.crc32(name.encode()), seed]).standard_normal(out[name].shape)
        drawn = base * np.exp(spread * noise) if base else spread * noise
        out[name] = jnp.asarray(drawn.astype(out[name].dtype))
    for name, factor in factors.items():
        out[name] = (out[name] * factor).astype(out[name].dtype)
    return out
```

```python
import numpy as np
import concourse.bass as bass
from concourse import mybir
from contextlib import ExitStack


def gated_xattn_moe_block(nc, x, ctx_rows, ctx_cols, gates, gate_w, bias, shared_up, shared_down, expert_w, out):
    fp32, bf16, u32, i32 = mybir.dt.float32, mybir.dt.bfloat16, mybir.dt.uint32, mybir.dt.int32
    ALU, ACT, AX = mybir.AluOpType, mybir.ActivationFunctionType, mybir.AxisListType

    P = 128
    D = 256
    S = 64
    E, G, K = 32, 8, 4
    EG = E // G
    TOKENS = x.shape[0] * P * x.shape[2] // D
    TILES = TOKENS // P
    J = 4
    GROUPS = TILES // J
    TG = J * P
    HS = 512
    HC = HS // P
    DC = D // P
    ROW = D + E
    EPS = 1e-5
    ROUTED_SCALE = 2.5
    BIG, LOW = 3.0e38, -3.0e38
    RING = 4

    tok_rows = nc.dram_tensor("tok_rows", (TOKENS + P, ROW), fp32, kind="Internal").ap()
    res_rows = nc.dram_tensor("res_rows", (TOKENS + P, D), fp32, kind="Internal").ap()

    ctx = ExitStack()
    with ctx:
        def sb(name, shape, dt=fp32):
            return ctx.enter_context(nc.sbuf_tensor(name, shape, dt))

        def sem(name):
            return ctx.enter_context(nc.semaphore(name))

        def wait(eng, semaphore, value):
            if not isinstance(value, int) or value > 0:
                eng.wait_ge(semaphore, value)

        def wait_apart(eng, semaphore, value):
            eng.wait_ge(semaphore, value)
            eng.sem_inc(waits_carried, 1)

        def span(first, end, step):
            return first, end - step + 1, step

        ident = sb("ident", [P, P])
        tri = sb("tri", [P, P], bf16)
        ones = sb("ones", [P, P], bf16)
        slot_col = sb("slot_col", [P, 1])
        slot_row = sb("slot_row", [P, P])
        restart = sb("restart", [P, E, TILES])
        one1 = sb("one1", [1, 1])
        minus_half = sb("minus_half", [P, J])
        zeros = sb("zeros", [P, ROW])
        biasb = sb("biasb", [P, E])
        gin = sb("gin", [P, 2])
        tg = sb("tg", [P, 2])
        wscale = sb("wscale", [P, 1])
        gwT = sb("gwT", [P, DC, E])
        suT = sb("suT", [P, DC, HS])
        sdT = sb("sdT", [P, HC, D])

        x4 = [sb(f"x4_{i}", [P, J, D]) for i in range(2)]
        c4 = [sb(f"c4_{i}", [P, J, D]) for i in range(2)]
        ct4 = [sb(f"ct4_{i}", [P, J, DC, P]) for i in range(2)]
        q4 = [sb(f"q4_{i}", [P, J, D]) for i in range(2)]
        sig_all = sb("sig_all", [P, 2, 2, DC, D])
        sig = [sig_all[:, i] for i in range(2)]
        x1 = [sb(f"x1_{i}", [P, J, D]) for i in range(2)]
        rows = [sb(f"rows_{i}", [P, J, ROW]) for i in range(2)]
        xt4 = [sb(f"xt4_{i}", [P, DC, TG]) for i in range(2)]
        xt_all = sb("xt_all", [P, DC, TOKENS])
        stats1 = sb("stats1", [P, J, 6])
        mv1 = [sb(f"mv1_{i}", [P, J, 2]) for i in range(2)]
        ve1 = sb("ve1", [P, J])
        rstd1 = [sb(f"rstd1_{i}", [P, J]) for i in range(2)]
        stats2 = sb("stats2", [P, J, 6])
        mv2 = [sb(f"mv2_{i}", [P, J, 2]) for i in range(2)]
        ve2 = sb("ve2", [P, J])
        rstd2 = [sb(f"rstd2_{i}", [P, J]) for i in range(2)]
        scores = [sb(f"scores_{i}", [P, J, E]) for i in range(2)]
        biased = sb("biased", [P, J, E])
        pair_hi = sb("pair_hi", [P, J * G, 2])
        pair_lo = sb("pair_lo", [P, J * G, 2])
        top1 = sb("top1", [P, J * G])
        mid = sb("mid", [P, J * G])
        top2 = sb("top2", [P, J * G])
        group_in = sb("group_in", [P, J, G + K])
        group_top = sb("group_top", [P, J, 8])
        group_rep = sb("group_rep", [P, J, 8])
        group_out = sb("group_out", [P, J, G + K])
        group_sel = sb("group_sel", [P, J * G])
        masked = sb("masked", [P, J * G, EG])
        exp_in = sb("exp_in", [P, J, E + K])
        exp_top = sb("exp_top", [P, J, 8])
        exp_rep = sb("exp_rep", [P, J, 8])
        exp_out = sb("exp_out", [P, J, E + K])
        picked = sb("picked", [P, J, E])
        pick_sum = sb("pick_sum", [P, J])
        pick_inv = sb("pick_inv", [P, J])
        sel_all = sb("sel_all", [P, TILES, E], bf16)

        relu_h = [sb(f"relu_h_{i}", [P, TG]) for i in range(2)]
        hT = sb("hT", [P, HC, TG])
        y_all = sb("y_all", [P, TILES, D])
        upto = sb("upto", [P, E, TILES])
        upto_excl = sb("upto_excl", [1, E, TILES])
        before = sb("before", [P, E, TILES])
        before_n = sb("before_n", [P, E, TILES])
        tile_of = sb("tile_of", [P, E])
        base_of = sb("base_of", [P, E])
        rank = sb("rank", [P, E])
        bounds = sb("bounds", [P, 2, 8])
        from_lo = q4[0][:, :, :].rearrange("p j (k q) -> p (j k) q", q=P)
        from_hi = q4[1][:, :, :].rearrange("p j (k q) -> p (j k) q", q=P)
        onehot = sb("onehot", [P, 8, P], bf16)
        prefix = sb("prefix", [P, 8, P], bf16)
        cmp = sig_all[:, :, :, :, :].rearrange("p i b c (h q) -> p (i b c h) q", q=P)
        in_tile = sb("in_tile", [P, E])
        valid = sb("valid", [P, E])
        tok_a = sb("tok_a", [P, E])
        tok_b = sb("tok_b", [P, E])
        tok_c = sb("tok_c", [P, E])
        tok_id = sb("tok_id", [P, E], u32)
        slot_tok = sb("slot_tok", [P, 8], u32)
        wring = [sb(f"wring_{i}", [P, 2 * D]) for i in range(RING)]
        xe = [sb(f"xe_{i}", [P, ROW]) for i in range(RING)]
        xeT = [sb(f"xeT_{i}", [P, DC, P]) for i in range(2)]
        relu_e = sb("relu_e", [P, P])
        h_e = [sb(f"h_e_{i}", [P, P]) for i in range(2)]
        y_e = [sb(f"y_e_{i}", [P, D]) for i in range(2)]
        fin = x4

        psum = ctx.enter_context(nc.psum_tensor("psum", [P, 8 * 512], fp32))
        bank = [psum[:, 512 * i:512 * i + 512] for i in range(8)]
        logits = [psum[:, 1024 * i:1024 * i + 1024] for i in range(2)]

        waits_carried = sem("waits_carried")
        params_loaded = sem("params_loaded")
        shared_loaded = sem("shared_loaded")
        dump_rows_zeroed = sem("dump_rows_zeroed")
        pool_self = sem("pool_self")
        consts_ready = sem("consts_ready")
        zeros_ready = sem("zeros_ready")
        marks_ready = sem("marks_ready")
        tanh_ready = sem("tanh_ready")
        inputs_loaded = [sem(f"inputs_loaded_{i}") for i in range(2)]
        stats1_ready = sem("stats1_ready")
        rstd1_ready = sem("rstd1_ready")
        q_ready = sem("q_ready")
        logits_ready = sem("logits_ready")
        sig_ready = sem("sig_ready")
        pv_ready = sem("pv_ready")
        x1_ready = sem("x1_ready")
        stats2_ready = sem("stats2_ready")
        rstd2_ready = sem("rstd2_ready")
        xn_ready = sem("xn_ready")
        xt_in_psum = sem("xt_in_psum")
        xt_ready = sem("xt_ready")
        gate_ready = sem("gate_ready")
        scores_ready = sem("scores_ready")
        routed = sem("routed")
        x1_stored = [sem(f"x1_stored_{i}") for i in range(2)]
        rows_stored = [sem(f"rows_stored_{i}") for i in range(2)]
        dve_self = sem("dve_self")
        totals_ready = sem("totals_ready")
        prefix_ready = sem("prefix_ready")
        scan_ready = sem("scan_ready")
        bounds_in_psum = sem("bounds_in_psum")
        onehot_ready = sem("onehot_ready")
        prefix_copied = sem("prefix_copied")
        counts_ready = sem("counts_ready")
        counts_read = sem("counts_read")
        table_ready = sem("table_ready")
        up_ready = sem("up_ready")
        relu_done = sem("relu_done")
        h_ready = sem("h_ready")
        y_ready = sem("y_ready")
        y_kept = sem("y_kept")
        weights_loaded = [sem(f"weights_loaded_{i}") for i in range(RING)]
        gathered = [sem(f"gathered_{i}") for i in range(RING)]
        xe_in_psum = sem("xe_in_psum")
        xeT_ready = sem("xeT_ready")
        he_in_psum = sem("he_in_psum")
        he_read = sem("he_read")
        he_ready = sem("he_ready")
        ye_in_psum = sem("ye_in_psum")
        ye_ready = sem("ye_ready")
        scattered = sem("scattered")
        res_loaded = [sem(f"res_loaded_{i}") for i in range(2)]
        fin_ready = sem("fin_ready")
        out_stored = [sem(f"out_stored_{i}") for i in range(2)]

        block = ctx.enter_context(nc.Block())

        tok_groups = tok_rows[0:TOKENS].rearrange("(g j p) d -> g p j d", j=J, p=P)
        res_groups = res_rows[0:TOKENS].rearrange("(g j p) d -> g p j d", j=J, p=P)

        STEPS = GROUPS + 2

        def steps_of_a(eng, step):
            step(0, 0, (True, False, False))
            step(1, 1, (True, True, False))
            with eng.Fori(*span(2, GROUPS, 2)) as s:
                for h in range(2):
                    step(s + h, h, (True, True, True))
            step(GROUPS, 0, (False, True, True))
            step(GROUPS + 1, 1, (False, False, True))

        def nth(b, par):
            return b - par

        @block.sync
        def _(sp):
            def load(b, par):
                g = bass.ds(b, 1)
                sp.dma_start(x4[par][:, :, :].rearrange("p j d -> p (j d)"), x[g].rearrange("g p f -> p (g f)")).then_inc(inputs_loaded[par], 16)
                sp.dma_start(c4[par][:, :, :].rearrange("p j d -> p (j d)"), ctx_rows[g].rearrange("g p f -> p (g f)")).then_inc(inputs_loaded[par], 16)
                sp.dma_start(ct4[par][:, :, :, :].rearrange("p j c d -> p (j c d)"), ctx_cols[g].rearrange("g p f -> p (g f)")).then_inc(inputs_loaded[par], 16)

            load(0, 0)
            sp.dma_start(gin[:, :], gates).then_inc(params_loaded, 16)
            sp.dma_start(biasb[:, :], bias).then_inc(params_loaded, 16)
            sp.dma_start(gwT[:, :, :].rearrange("p c e -> p (c e)"), gate_w).then_inc(params_loaded, 16)
            load(1, 1)
            sp.wait_ge(zeros_ready, 1)
            sp.dma_start(tok_rows[TOKENS:TOKENS + P], zeros[:, :]).then_inc(dump_rows_zeroed, 16)
            sp.dma_start(res_rows[TOKENS:TOKENS + P], zeros[:, 0:D]).then_inc(dump_rows_zeroed, 16)
            sp.dma_start(suT[:, :, :].rearrange("p c e -> p (c e)"), shared_up).then_inc(shared_loaded, 16)
            sp.dma_start(sdT[:, :, :].rearrange("p c e -> p (c e)"), shared_down).then_inc(shared_loaded, 16)

            def store_x1(b, par):
                sp.wait_ge(x1_ready, J * b + J)
                sp.dma_start(res_groups[bass.ds(b, 1)].rearrange("g p j d -> p (g j) d"), x1[par][:, :, :]).then_inc(x1_stored[par], 16)

            def store_rows(b, par):
                sp.wait_ge(routed, b + 1)
                sp.dma_start(tok_groups[bass.ds(b, 1)].rearrange("g p j d -> p (g j) d"), rows[par][:, :, :]).then_inc(rows_stored[par], 16)

            def step(s, h, live):
                now, prev, prev2 = live
                if prev:
                    store_x1(s - 1, 1 - h)
                    if not isinstance(s, int) or s + 1 < GROUPS:
                        load(s + 1, 1 - h)
                if prev2:
                    store_rows(s - 2, h)

            step(0, 0, (True, False, False))
            step(1, 1, (True, True, False))
            with sp.Fori(*span(2, GROUPS - 2, 2)) as s:
                for h in range(2):
                    step(s + h, h, (True, True, True))
            step(GROUPS - 2, 0, (True, True, True))
            step(GROUPS - 1, 1, (True, True, True))
            step(GROUPS, 0, (False, True, True))
            step(GROUPS + 1, 1, (False, False, True))

            def load_weights(e, r):
                sp.dma_start(wring[r][:, :], expert_w[bass.ds(e, 1)].rearrange("e p f -> p (e f)")).then_inc(weights_loaded[r], 16)

            for r in range(RING):
                load_weights(r, r)
            with sp.Fori(*span(0, E - RING, RING)) as e0:
                for r in range(RING):
                    sp.wait_ge(ye_in_psum, e0 + r + 1)
                    load_weights(e0 + r + RING, r)

            sp.wait_ge(scattered, 16 * E)
            def load_res(n, par):
                sp.dma_start(fin[par][:, :, :], res_groups[bass.ds(n, 1)].rearrange("g p j d -> p (g j) d")).then_inc(res_loaded[par], 16)

            def store_out(n, par):
                sp.wait_ge(fin_ready, n + 1)
                sp.dma_start(out[bass.ds(n, 1)].rearrange("g p f -> p (g f)"), fin[par][:, :, :].rearrange("p j d -> p (j d)")).then_inc(out_stored[par], 16)

            load_res(0, 0)
            load_res(1, 1)
            with sp.Fori(*span(0, GROUPS - 2, 2)) as n:
                for h in range(2):
                    store_out(n + h, h)
                    sp.wait_ge(out_stored[h], 8 * n + 16)
                    load_res(n + h + 2, h)
            for h in range(2):
                store_out(GROUPS - 2 + h, h)
            for h in range(2):
                sp.wait_ge(out_stored[h], 16 * GROUPS // 2)

        @block.gpsimd
        def _(pool):
            pool.memset(zeros[:, :], 0.0).then_inc(zeros_ready, 1)
            pool.memset(ident[:, :], 0.0).then_inc(pool_self, 1)
            pool.memset(minus_half[:, :], -0.5).then_inc(pool_self, 1)
            pool.wait_ge(pool_self, 2)
            pool.affine_select(out=ident[:, :], in_=ident[:, :], compare_op=ALU.not_equal, fill=1.0, base=0,
                               pattern=[[-1, P]], channel_multiplier=1).then_inc(consts_ready, 1)
            pool.memset(ones[:, :], 1.0).then_inc(consts_ready, 1)
            pool.memset(one1[:, :], 1.0).then_inc(consts_ready, 1)
            pool.wait_ge(consts_ready, 2)
            pool.affine_select(out=tri[:, :], in_=ones[:, :], compare_op=ALU.is_ge, fill=0.0, base=0,
                               pattern=[[1, P]], channel_multiplier=-1).then_inc(consts_ready, 1)
            pool.iota(slot_col[:, :], pattern=[[0, 1]], base=0, channel_multiplier=1,
                      allow_small_or_imprecise_dtypes=True).then_inc(consts_ready, 1)
            pool.iota(slot_row[:, :], pattern=[[1, P]], base=0, channel_multiplier=0,
                      allow_small_or_imprecise_dtypes=True).then_inc(consts_ready, 1)

            def inverse_root(b, par, mv, ve, rstd, stats_ready, ready):
                wait_apart(pool, stats_ready, b + 1)
                pool.tensor_scalar(ve[:, :], mv[par][:, :, 1], EPS, None, op0=ALU.add).then_inc(pool_self, 1)
                return lambda count: (pool.wait_ge(pool_self, count),
                                      pool.tensor_tensor(rstd[par][:, :], ve[:, :], minus_half[:, :], ALU.pow).then_inc(ready, 1))

            def norm1(b, par):
                inverse_root(b, par, mv1, ve1, rstd1, stats1_ready, rstd1_ready)(2 * b + 3)

            def norm2(b, par):
                inverse_root(b, par, mv2, ve2, rstd2, stats2_ready, rstd2_ready)(2 * b + 5)

            norm1(0, 0)
            pool.memset(restart[:, :, :], 1.0).then_inc(consts_ready, 1)
            pool.wait_ge(consts_ready, 7)
            pool.memset(restart[:, :, 0:1], 0.0).then_inc(consts_ready, 1)
            with pool.Fori(*span(0, GROUPS - 2, 2)) as b:
                for h in range(2):
                    inverse_root(b + h + 1, 1 - h, mv1, ve1, rstd1, stats1_ready, rstd1_ready)(2 * (b + h) + 4)
                    norm2(b + h, h)
            inverse_root(GROUPS - 1, 1, mv1, ve1, rstd1, stats1_ready, rstd1_ready)(2 * (GROUPS - 2) + 4)
            norm2(GROUPS - 2, 0)
            inverse_root(GROUPS - 1, 1, mv2, ve2, rstd2, stats2_ready, rstd2_ready)(2 * GROUPS + 2)

            idx_before = 2 * GROUPS + 2

            def gather(e, r):
                pool.tensor_copy(slot_tok[:, r % 8:r % 8 + 1], tok_id[:, bass.ds(e, 1)]).then_inc(pool_self, 1)
                wait_apart(pool, pool_self, idx_before + e + 1)
                pool.indirect_dma_start(xe[r % RING][:, :], None, tok_rows,
                                        bass.IndirectOffsetOnAxis(ap=slot_tok[:, r % 8:r % 8 + 1], axis=0)).then_inc(gathered[r % RING], 16)

            def scatter(e, r):
                wait_apart(pool, ye_ready, e + 1)
                pool.indirect_dma_start(res_rows, bass.IndirectOffsetOnAxis(ap=slot_tok[:, r % 8:r % 8 + 1], axis=0),
                                        y_e[r % 2][:, :], None, compute_op=ALU.add).then_inc(scattered, 16)

            pool.wait_ge(table_ready, 1)
            pool.wait_ge(dump_rows_zeroed, 32)
            for par in range(2):
                pool.wait_ge(rows_stored[par], 16 * GROUPS // 2)
                pool.wait_ge(x1_stored[par], 16 * GROUPS // 2)
            for r in range(RING):
                gather(r, r)

            def slots(e0, last_):
                for r in range(8):
                    scatter(e0 + r, r)
                    if not (last_ and r >= 8 - RING):
                        gather(e0 + r + RING, r + RING)
                    wait_apart(pool, scattered, 16 * e0 + 16 * (r + 1))

            with pool.Fori(*span(0, E - 8, 8)) as e0:
                slots(e0, False)
            slots(E - 8, True)

        @block.scalar
        def _(act):
            act.wait_ge(params_loaded, 48)
            nc.scalar.activation(tg[:, :], gin[:, :], ACT.Tanh).then_inc(tanh_ready, 1)

            def sigmoid(s, j):
                t = s * J + j
                act.wait_ge(logits_ready, t + 1)
                wait(act, pv_ready, t - 1)
                nc.scalar.activation(sig[j % 2][:, :, :, :].rearrange("p b c m -> p (b c m)"), logits[j % 2], ACT.Sigmoid,
                                     scale=float(S) ** -0.5).then_inc(sig_ready, 1)

            def copy_xt(b, par, dc):
                act.wait_ge(xt_in_psum, 2 * b + dc + 1)
                nc.scalar.copy(xt4[par][:, dc, :], bank[6][:, :])
                nc.scalar.copy(xt_all[:, dc, bass.ds(b * TG, TG)], bank[6][:, :]).then_inc(xt_ready, 1)

            def score(b, par):
                act.wait_ge(gate_ready, b + 1)
                nc.scalar.activation(scores[par][:, :, :].rearrange("p j e -> p (j e)"), bank[7][:, 0:J * E],
                                     ACT.Sigmoid).then_inc(scores_ready, 1)

            def step(s, h, live):
                now, prev, prev2 = live
                if now:
                    sigmoid(s, 0)
                    sigmoid(s, 1)
                if prev2:
                    score(s - 2, h)
                if now:
                    sigmoid(s, 2)
                if prev:
                    copy_xt(s - 1, 1 - h, 0)
                if now:
                    sigmoid(s, 3)
                if prev:
                    copy_xt(s - 1, 1 - h, 1)

            steps_of_a(act, step)

            def up_chunk(n, c):
                u = HC * n + c
                act.wait_ge(up_ready, u + 1)
                nc.scalar.activation(relu_h[c % 2][:, :], bank[c % 2][:, :], ACT.Relu).then_inc(relu_done, 1)
                act.wait_ge(relu_done, u + 1)
                nc.scalar.activation(hT[:, c, :], relu_h[c % 2][:, :], ACT.Square).then_inc(h_ready, 1)

            def down_tile(n, j):
                t = J * n + j
                act.wait_ge(y_ready, t + 1)
                nc.scalar.activation(y_all[:, bass.ds(t, 1), :].rearrange("p t d -> p (t d)"), bank[2 + j % 2][:, 0:D],
                                     ACT.Copy, scale=tg[:, 1:2]).then_inc(y_kept, 1)

            with act.Fori(0, GROUPS) as n:
                for c in range(HC):
                    up_chunk(n, c)
                for j in range(J):
                    down_tile(n, j)

        @block.tensor
        def _(pe):
            pe.wait_ge(consts_ready, 6)

            def qk(s, h, j):
                t = s * J + j
                if j == 0:
                    pe.wait_ge(inputs_loaded[h], 24 * nth(s, h) + 48)
                    pe.wait_ge(q_ready, s + 1)
                wait(pe, sig_ready, t - 1)
                for half in range(DC):
                    for b in range(2):
                        rowsl = slice(S * b, S * b + S)
                        last = nc.tensor.matmul(bank[2 * (j % 2) + b][:, half * D:half * D + D],
                                                q4[h][rowsl, j, half * P:half * P + P], c4[h][rowsl, j, :],
                                                start=True, stop=True)
                last.then_inc(logits_ready, 1)

            def pv(s, h, j):
                t = s * J + j
                pe.wait_ge(sig_ready, t + 1)
                wait(pe, x1_ready, t - 1)
                for half in range(DC):
                    for b in range(2):
                        last = nc.tensor.matmul(bank[4 + j % 2][S * b:S * b + S, 0:D],
                                                ct4[h][:, j, half, S * b:S * b + S], sig[j % 2][:, b, half, :],
                                                start=(half == 0), stop=(half == DC - 1))
                last.then_inc(pv_ready, 1)

            def transpose_rows(b, par, dc):
                pe.wait_ge(xn_ready, b + 1)
                wait(pe, xt_ready, 2 * b + dc)
                for j in range(J):
                    last = nc.tensor.transpose(bank[6][:, j * P:j * P + P], rows[par][:, j, dc * P:dc * P + P], ident[:, :])
                last.then_inc(xt_in_psum, 1)

            def gate(b, par):
                pe.wait_ge(xt_ready, 2 * b + 2)
                for j in range(J):
                    for dc in range(DC):
                        last = nc.tensor.matmul(bank[7][:, j * E:j * E + E], xt4[par][:, dc, j * P:j * P + P],
                                                gwT[:, dc, :], start=(dc == 0), stop=(dc == DC - 1))
                last.then_inc(gate_ready, 1)

            def step(s, h, live):
                now, prev, prev2 = live
                if now:
                    qk(s, h, 0)
                if prev:
                    pv(s - 1, 1 - h, J - 1)
                if now:
                    qk(s, h, 1)
                    pv(s, h, 0)
                if prev2:
                    gate(s - 2, h)
                if now:
                    qk(s, h, 2)
                    pv(s, h, 1)
                if prev:
                    transpose_rows(s - 1, 1 - h, 0)
                if now:
                    qk(s, h, 3)
                    pv(s, h, 2)
                if prev:
                    transpose_rows(s - 1, 1 - h, 1)

            pe.wait_ge(params_loaded, 48)
            steps_of_a(pe, step)

            def totals():
                pe.wait_ge(routed, GROUPS)
                pe.wait_ge(pv_ready, TILES)
                for half in range(2):
                    lo = half * (TILES // 2)
                    last = nc.tensor.matmul(bank[4 + half][:, :], ones[:, :],
                                            sel_all[:, lo:lo + TILES // 2, :].rearrange("p i e -> p (i e)"), start=True, stop=True)
                last.then_inc(totals_ready, 1)
                pe.wait_ge(xt_ready, 2 * GROUPS)
                for k in range(8):
                    for q in range(4):
                        last = nc.tensor.matmul(bank[6 + k // 4][32 * q:32 * q + 32, (k % 4) * P:(k % 4) * P + P],
                                                sel_all[:, :, 4 * k + q], tri[:, :], start=True, stop=True,
                                                tile_position=(0, 32 * q))
                last.then_inc(prefix_ready, 1)

            def bounds_up():
                pe.wait_ge(scan_ready, 1)
                for hi in range(2):
                    for k in range(8):
                        row = (upto if hi else upto_excl)[0:1, 4 * k:4 * k + 4, :].rearrange("p e i -> p (e i)")
                        last = nc.tensor.matmul(bank[4][:, hi * 8 + k:hi * 8 + k + 1], row, one1[0:1, 0:1], start=True, stop=True)
                last.then_inc(bounds_in_psum, 1)

            def counts(r):
                if r == 0:
                    pe.wait_ge(onehot_ready, 1)
                    pe.wait_ge(prefix_copied, 1)
                else:
                    pe.wait_ge(counts_read, 1)
                for q in range(4):
                    for k in range(4):
                        kk = 4 * r + k
                        last = nc.tensor.matmul(bank[4 + q][:, k * P:k * P + P], onehot[32 * q:32 * q + 32, kk, :],
                                                prefix[32 * q:32 * q + 32, kk, :], start=True, stop=True,
                                                tile_position=(32 * q, 0))
                last.then_inc(counts_ready, 1)

            def up_chunk(n, c):
                u = HC * n + c
                wait(pe, h_ready, u - 1)
                for dc in range(DC):
                    last = nc.tensor.matmul(bank[c % 2][:, :], suT[:, dc, c * P:c * P + P],
                                            xt_all[:, dc, bass.ds(n * TG, TG)], start=(dc == 0), stop=(dc == DC - 1))
                last.then_inc(up_ready, 1)

            def down_tile(n, j):
                t = J * n + j
                pe.wait_ge(h_ready, HC * n + HC)
                wait(pe, y_kept, t - 1)
                for c in range(HC):
                    last = nc.tensor.matmul(bank[2 + j % 2][:, 0:D], hT[:, c, j * P:j * P + P], sdT[:, c, :],
                                            start=(c == 0), stop=(c == HC - 1))
                last.then_inc(y_ready, 1)

            def shared_piece(n, k):
                up_chunk(n, k) if k < HC else down_tile(n, k - HC)

            def rows_T(e, r):
                pe.wait_ge(gathered[r % RING], 16 * ((e - r % RING) // RING) + 16 if isinstance(e, int) else 4 * (e - r % RING) + 16)
                wait(pe, xeT_ready, e)
                for dc in range(DC):
                    last = nc.tensor.transpose(bank[4][:, dc * P:dc * P + P], xe[r % RING][:, dc * P:dc * P + P], ident[:, :])
                last.then_inc(xe_in_psum, 1)

            def expert_up(e, r):
                pe.wait_ge(weights_loaded[r % RING], 16 * ((e - r % RING) // RING) + 16 if isinstance(e, int) else 4 * (e - r % RING) + 16)
                pe.wait_ge(xeT_ready, e + 1)
                wait(pe, he_ready, e)
                for dc in range(DC):
                    last = nc.tensor.matmul(bank[5][:, 0:P], wring[r % RING][:, dc * P:dc * P + P], xeT[r % 2][:, dc, :],
                                            start=(dc == 0), stop=(dc == DC - 1))
                last.then_inc(he_in_psum, 1)

            def expert_down(e, r):
                pe.wait_ge(he_ready, e + 1)
                wait(pe, ye_ready, e)
                nc.tensor.matmul(bank[6][:, 0:D], h_e[r % 2][:, :], wring[r % RING][:, D:2 * D],
                                 start=True, stop=True).then_inc(ye_in_psum, 1)

            pe.wait_ge(shared_loaded, 32)
            totals()
            shared_piece(0, 0)
            bounds_up()
            for k in range(1, 5):
                shared_piece(0, k)
            counts(0)
            for k in range(5, 8):
                shared_piece(0, k)
            counts(1)
            for k in range(8):
                shared_piece(1, k)

            rows_T(0, 0)

            def slots(n, e0, first, last_):
                for k in range(8):
                    e = e0 + k
                    expert_up(e, k)
                    if not (last_ and k == 7):
                        rows_T(e + 1, k + 1)
                    if not (first and k == 0):
                        expert_down(e - 1, k + 7)
                    shared_piece(n, k)

            slots(2, 0, True, False)
            with pe.Fori(3, 5) as n:
                slots(n, n * 8 - 16, False, False)
            slots(5, E - 8, False, True)
            expert_down(E - 1, 7)
            with pe.Fori(6, GROUPS) as n:
                for k in range(8):
                    shared_piece(n, k)

        @block.vector
        def _(dve):
            V = nc.vector

            class Own:
                def __init__(self):
                    self.base, self.n = 0, 0

                def mark(self, instruction):
                    instruction.then_inc(dve_self, 1)
                    self.n += 1

                def wait(self):
                    dve.wait_ge(dve_self, self.base + self.n)

                def wait_apart(self):
                    wait_apart(dve, dve_self, self.base + self.n)

            own = Own()

            own.mark(V.memset(group_in[:, :, :], LOW))
            own.mark(V.memset(group_rep[:, :, :], LOW))
            own.mark(V.memset(exp_in[:, :, :], LOW))
            own.mark(V.memset(exp_rep[:, :, :], LOW))

            def norm1_stats(b, par):
                dve.wait_ge(inputs_loaded[par], 24 * nth(b, par) + 48)
                for j in range(J):
                    own.mark(V.bn_stats(stats1[:, j, :], x4[par][:, j, :]))
                own.wait_apart()
                for j in range(J):
                    last = V.bn_aggr(mv1[par][:, j, :], stats1[:, j, :])
                last.then_inc(stats1_ready, 1)

            def norm1_apply(b, par):
                dve.wait_ge(rstd1_ready, b + 1)
                for j in range(J):
                    last = V.tensor_scalar(q4[par][:, j, :], x4[par][:, j, :], mv1[par][:, j, 0:1], rstd1[par][:, j:j + 1],
                                           op0=ALU.subtract, op1=ALU.mult)
                last.then_inc(q_ready, 1)

            def residual(s, h, j):
                t = s * J + j
                dve.wait_ge(pv_ready, t + 1)
                if j == 0 and (not isinstance(s, int) or s >= 2):
                    dve.wait_ge(x1_stored[h], 8 * nth(s, h))
                V.scalar_tensor_tensor(x1[h][:, j, :], bank[4 + j % 2][:, 0:D], tg[:, 0:1], x4[h][:, j, :],
                                       op0=ALU.mult, op1=ALU.add).then_inc(x1_ready, 1)
                dve.wait_ge(x1_ready, t + 1)
                own.mark(V.bn_stats(stats2[:, j, :], x1[h][:, j, :]))
                if j == J - 1:
                    own.wait_apart()
                    for k in range(J):
                        last = V.bn_aggr(mv2[h][:, k, :], stats2[:, k, :])
                    last.then_inc(stats2_ready, 1)

            def norm2_apply(b, par):
                dve.wait_ge(rstd2_ready, b + 1)
                if not isinstance(b, int) or b >= 2:
                    dve.wait_ge(rows_stored[par], 8 * nth(b, par))
                    dve.wait_ge(xt_in_psum, 2 * b - 2)
                for j in range(J):
                    last = V.tensor_scalar(rows[par][:, j, 0:D], x1[par][:, j, :], mv2[par][:, j, 0:1], rstd2[par][:, j:j + 1],
                                           op0=ALU.subtract, op1=ALU.mult)
                last.then_inc(xn_ready, 1)

            def route(b, par):
                dve.wait_ge(scores_ready, b + 1)
                sc = scores[par]

                def do(instruction):
                    own.mark(instruction)
                    own.wait()
                do(V.tensor_tensor(biased[:, :, :], sc[:, :, :], biasb[:, :].unsqueeze(1).to_broadcast([P, J, E]), ALU.add))
                bv = biased[:, :, :].rearrange("p j (g a b) -> p (j g) a b", g=G, a=2)
                own.mark(V.tensor_tensor(pair_hi[:, :, :], bv[:, :, :, 0], bv[:, :, :, 1], ALU.max))
                do(V.tensor_tensor(pair_lo[:, :, :], bv[:, :, :, 0], bv[:, :, :, 1], ALU.min))
                own.mark(V.tensor_tensor(top1[:, :], pair_hi[:, :, 0], pair_hi[:, :, 1], ALU.max))
                own.mark(V.tensor_tensor(mid[:, :], pair_hi[:, :, 0], pair_hi[:, :, 1], ALU.min))
                do(V.tensor_tensor(top2[:, :], pair_lo[:, :, 0], pair_lo[:, :, 1], ALU.max))
                do(V.tensor_tensor(mid[:, :], mid[:, :], top2[:, :], ALU.max))
                own.mark(V.tensor_tensor(group_in[:, :, 0:G], top1[:, :].rearrange("p (j g) -> p j g", g=G),
                                         mid[:, :].rearrange("p (j g) -> p j g", g=G), ALU.add))
                own.wait_apart()
                for j in range(J):
                    own.mark(V.max(group_top[:, j, :], group_in[:, j, 0:G]))
                own.wait()
                own.mark(V.tensor_copy(group_rep[:, :, 0:K], group_top[:, :, 0:K]))
                own.wait_apart()
                for j in range(J):
                    own.mark(V.match_replace(group_out[:, j, :], group_rep[:, j, :], group_in[:, j, :], BIG))
                own.wait()
                do(V.tensor_scalar(group_sel[:, :].rearrange("p (j g) -> p j g", g=G), group_out[:, :, 0:G], BIG / 2, None, op0=ALU.is_ge))
                do(V.tensor_tensor(masked[:, :, :], biased[:, :, :].rearrange("p j (g a) -> p (j g) a", g=G),
                                   group_sel[:, :].unsqueeze(2).to_broadcast([P, J * G, EG]), ALU.mult))
                own.mark(V.tensor_scalar(exp_in[:, :, 0:E], masked[:, :, :].rearrange("p (j g) a -> p j (g a)", j=J), 0.0, None, op0=ALU.add))
                own.wait_apart()
                for j in range(J):
                    own.mark(V.max(exp_top[:, j, :], exp_in[:, j, 0:E]))
                own.wait()
                own.mark(V.tensor_copy(exp_rep[:, :, 0:K], exp_top[:, :, 0:K]))
                own.wait_apart()
                for j in range(J):
                    own.mark(V.match_replace(exp_out[:, j, :], exp_rep[:, j, :], exp_in[:, j, :], BIG))
                own.wait()
                own.mark(V.tensor_scalar(sel_all[:, bass.ds(b * J, J), :], exp_out[:, :, 0:E], BIG / 2, None, op0=ALU.is_ge))
                do(V.scalar_tensor_tensor(picked[:, :, :], exp_out[:, :, 0:E], BIG / 2, sc[:, :, :], op0=ALU.is_ge, op1=ALU.mult))
                do(V.tensor_reduce(pick_sum[:, :], picked[:, :, :], AX.X, ALU.add))
                do(V.tensor_scalar(pick_sum[:, :], pick_sum[:, :], 1e-20, None, op0=ALU.add))
                do(V.reciprocal(pick_inv[:, :], pick_sum[:, :]))
                do(V.tensor_scalar(pick_inv[:, :], pick_inv[:, :], wscale[:, 0:1], None, op0=ALU.mult))
                V.tensor_tensor(rows[par][:, :, D:ROW], picked[:, :, :], pick_inv[:, :].unsqueeze(2).to_broadcast([P, J, E]),
                                ALU.mult).then_inc(routed, 1)

            def step(s, h, live):
                now, prev, prev2 = live
                if prev:
                    residual(s - 1, 1 - h, J - 1)
                if now and (not isinstance(s, int) or s + 1 < GROUPS):
                    norm1_stats(s + 1, 1 - h)
                if prev:
                    norm2_apply(s - 1, 1 - h)
                if now:
                    residual(s, h, 0)
                if now and (not isinstance(s, int) or s + 1 < GROUPS):
                    norm1_apply(s + 1, 1 - h)
                if prev2:
                    route(s - 2, h)
                if now:
                    residual(s, h, 1)
                    residual(s, h, 2)

            norm1_stats(0, 0)
            norm1_apply(0, 0)
            dve.wait_ge(tanh_ready, 1)
            own.mark(V.tensor_scalar(wscale[:, :], tg[:, 1:2], ROUTED_SCALE, None, op0=ALU.mult))
            step(0, 0, (True, False, False))
            step(1, 1, (True, True, False))
            PER_STEP = 43
            start = own.n
            with dve.Fori(*span(2, GROUPS - 2, 2)) as s:
                own.base, own.n = (s - 2) * PER_STEP + start, 0
                for h in range(2):
                    step(s + h, h, (True, True, True))
                assert own.n == 2 * PER_STEP, own.n
            own.base, own.n = 0, start + (GROUPS - 4) * PER_STEP
            step(GROUPS - 2, 0, (True, True, True))
            step(GROUPS - 1, 1, (True, True, True))
            step(GROUPS, 0, (False, True, True))
            step(GROUPS + 1, 1, (False, False, True))

            def do(instruction):
                own.mark(instruction)
                own.wait()
            dve.wait_ge(consts_ready, 8)
            dve.wait_ge(totals_ready, 1)
            for half in range(2):
                i0 = half * (TILES // 2)
                own.mark(V.tensor_copy(before_n[:, :, i0:i0 + TILES // 2],
                                       bank[4 + half][:, :].rearrange("p (i e) -> p e i", e=E)))
            own.wait()
            own.mark(V.tensor_tensor_scan(upto[:, :, :].rearrange("p e i -> p (e i)"), restart[:, :, :].rearrange("p e i -> p (e i)"),
                                          before_n[:, :, :].rearrange("p e i -> p (e i)"), 0.0, ALU.mult, ALU.add))
            own.wait()
            V.tensor_tensor(upto_excl[0:1, :, :], upto[0:1, :, :], before_n[0:1, :, :], ALU.subtract).then_inc(scan_ready, 1)
            dve.wait_ge(scan_ready, 1)
            tot = upto[:, :, :]
            do(V.tensor_scalar(before[:, :, :], tot, slot_col[:, 0:1], None, op0=ALU.is_le))
            dve.wait_ge(prefix_ready, 1)
            for half in range(2):
                last = V.tensor_copy(prefix[:, 4 * half:4 * half + 4, :].rearrange("p k q -> p (k q)"), bank[6 + half][:, :])
            last.then_inc(prefix_copied, 1)
            dve.wait_ge(bounds_in_psum, 1)
            do(V.tensor_copy(bounds[:, :, :].rearrange("p h k -> p (h k)"), bank[4][:, 0:16]))
            slotb = slot_row[:, :].unsqueeze(1).to_broadcast([P, 8, P])
            own.mark(V.tensor_tensor(from_lo[:, :, :], slotb, bounds[:, 0, :].unsqueeze(2).to_broadcast([P, 8, P]), ALU.is_ge))
            do(V.tensor_tensor(from_hi[:, :, :], slotb, bounds[:, 1, :].unsqueeze(2).to_broadcast([P, 8, P]), ALU.is_ge))
            V.tensor_tensor(onehot[:, :, :], from_lo[:, :, :], from_hi[:, :, :], ALU.subtract).then_inc(onehot_ready, 1)
            own.mark(V.tensor_reduce(tile_of[:, :], before[:, :, :], AX.X, ALU.add))
            do(V.tensor_tensor(before_n[:, :, :], before[:, :, :], tot, ALU.mult))
            do(V.tensor_reduce(base_of[:, :], before_n[:, :, :], AX.X, ALU.max))
            do(V.tensor_scalar(rank[:, :], base_of[:, :], -1.0, slot_col[:, 0:1], op0=ALU.mult, op1=ALU.add))
            for r in range(2):
                dve.wait_ge(counts_ready, r + 1)
                for q in range(4):
                    e0 = 16 * r + q
                    last = V.tensor_tensor(cmp[:, 4 * q:4 * q + 4, :], bank[4 + q][:, :].rearrange("p (k q) -> p k q", q=P),
                                           rank[:, e0:e0 + 13:4].unsqueeze(2).to_broadcast([P, 4, P]), ALU.is_le)
                    own.mark(last)
                own.wait()
                last = V.tensor_reduce(in_tile[:, 16 * r:16 * r + 16].rearrange("p (k q) -> p q k", q=4),
                                       cmp[:, :, :].rearrange("p (q k) t -> p q k t", q=4), AX.X, ALU.add)
                last.then_inc(counts_read, 1)
            dve.wait_ge(counts_read, 2)
            do(V.tensor_scalar(valid[:, :], tile_of[:, :], float(TILES), None, op0=ALU.is_lt))
            own.mark(V.tensor_tensor(tok_a[:, :], in_tile[:, :], valid[:, :], ALU.mult))
            do(V.tensor_scalar(tok_b[:, :], valid[:, :], -1.0, 1.0, op0=ALU.mult, op1=ALU.add))
            do(V.tensor_scalar(tok_c[:, :], tok_b[:, :], slot_col[:, 0:1], None, op0=ALU.mult))
            do(V.scalar_tensor_tensor(tok_b[:, :], tile_of[:, :], float(P), tok_a[:, :], op0=ALU.mult, op1=ALU.add))
            V.tensor_tensor(tok_id[:, :], tok_b[:, :], tok_c[:, :], ALU.add).then_inc(table_ready, 1)

            def copy_rows_T(e, r):
                dve.wait_ge(xe_in_psum, e + 1)
                wait(dve, he_in_psum, e - 1)
                V.tensor_copy(xeT[r % 2][:, :, :].rearrange("p c s -> p (c s)"), bank[4][:, 0:D]).then_inc(xeT_ready, 1)

            def hidden(e, r):
                dve.wait_ge(he_in_psum, e + 1)
                V.tensor_scalar(relu_e[:, :], bank[5][:, 0:P], 0.0, None, op0=ALU.max).then_inc(he_read, 1)
                dve.wait_ge(he_read, e + 1)
                wait(dve, ye_in_psum, e - 1)
                V.tensor_tensor(h_e[r % 2][:, :], relu_e[:, :], relu_e[:, :], ALU.mult).then_inc(he_ready, 1)

            def weigh(e, r):
                dve.wait_ge(ye_in_psum, e + 1)
                wait(dve, scattered, 16 * (e - 1))
                V.tensor_scalar(y_e[r % 2][:, :], bank[6][:, 0:D], xe[r % RING][:, bass.ds(e + D, 1)], None,
                                op0=ALU.mult).then_inc(ye_ready, 1)

            def slots(e0, first, last_):
                for k in range(8):
                    e = e0 + k
                    hidden(e, k)
                    if not (last_ and k == 7):
                        copy_rows_T(e + 1, k + 1)
                    if not (first and k == 0):
                        weigh(e - 1, k + 7)

            copy_rows_T(0, 0)
            slots(0, True, False)
            with dve.Fori(*span(8, E - 8, 8)) as e0:
                slots(e0, False, False)
            slots(E - 8, False, True)
            weigh(E - 1, 7)

            with dve.Fori(*span(0, GROUPS, 2)) as n:
                for h in range(2):
                    dve.wait_ge(res_loaded[h], 8 * n + 16)
                    dve.wait_ge(y_kept, J * n + J * h + J)
                    V.tensor_tensor(fin[h][:, :, :], fin[h][:, :, :], y_all[:, bass.ds(J * n + J * h, J), :],
                                    ALU.add).then_inc(fin_ready, 1)


_INS = ("x", "ctx_rows", "ctx_cols", "gates", "gate_w", "bias", "shared_up", "shared_down", "expert_w")


def kernel(x, ctx_2048, g_xattn, g_ffn, L0_ffn_gate_w, L0_ffn_bias_corr, L0_ffn_up_w, L0_ffn_down_w,
           L0_ffn_shared_up_w, L0_ffn_shared_down_w):
    import concourse.bacc as bacc
    from concourse.bass_utils import run_bass_kernel_spmd

    arr = lambda a: np.ascontiguousarray(np.asarray(a))
    x, c = np.asarray(x), np.asarray(ctx_2048)
    B, S, D = x.shape
    E, H, _ = L0_ffn_up_w.shape

    def groups(a):
        return arr(a.reshape(-1, 4, 128, D).transpose(0, 2, 1, 3).reshape(-1, 128, 4 * D))

    def cols(w):
        w = np.asarray(w)
        return arr(w.T.reshape(-1, 128, w.shape[0]).transpose(1, 0, 2).reshape(128, -1))

    ct = arr(c.reshape(-1, 4, 2, S, 2, 128).transpose(0, 5, 1, 4, 2, 3).reshape(-1, 128, 4 * 2 * 128))
    up = np.asarray(L0_ffn_up_w).transpose(0, 2, 1).reshape(E, 2, 128, H).transpose(0, 2, 1, 3).reshape(E, 128, 2 * H)
    down = np.asarray(L0_ffn_down_w).transpose(0, 2, 1)
    arrays = {
        "x": groups(x),
        "ctx_rows": groups(c),
        "ctx_cols": ct,
        "gates": arr(np.broadcast_to(np.stack([np.asarray(g_xattn)[0], np.asarray(g_ffn)[0]]), (128, 2))),
        "gate_w": cols(L0_ffn_gate_w),
        "bias": arr(np.broadcast_to(np.asarray(L0_ffn_bias_corr), (128, E))),
        "shared_up": cols(L0_ffn_shared_up_w),
        "shared_down": cols(L0_ffn_shared_down_w),
        "expert_w": arr(np.concatenate([up, down], axis=2)),
    }
    nc = bacc.Bacc("TRN2", target_bir_lowering=False, num_devices=1)
    aps = [nc.dram_tensor(n, arrays[n].shape, mybir.dt.float32, kind="ExternalInput").ap() for n in _INS]
    out = nc.dram_tensor("out", arrays["x"].shape, mybir.dt.float32, kind="ExternalOutput").ap()
    gated_xattn_moe_block(nc, *aps, out)
    r = run_bass_kernel_spmd(nc, [arrays], core_ids=[0])
    got = r.results[0]["out"]
    return arr(got.reshape(-1, 128, 4, D).transpose(0, 2, 1, 3).reshape(B, S, D))
```

```python
import numpy as np
import concourse.bass as bass
from concourse import mybir
from contextlib import ExitStack


def gated_xattn_moe_block(nc, x, ctx_rows, ctx_cols, gates, gate_w, bias, shared_up, shared_down, expert_w, out):
    fp32, bf16, u32, i32 = mybir.dt.float32, mybir.dt.bfloat16, mybir.dt.uint32, mybir.dt.int32
    ALU, ACT, AX = mybir.AluOpType, mybir.ActivationFunctionType, mybir.AxisListType

    P = 128
    D = 256
    S = 64
    E, G, K = 32, 8, 4
    EG = E // G
    TOKENS = x.shape[0] * P * x.shape[2] // D
    TILES = TOKENS // P
    J = 4
    GROUPS = TILES // J
    TG = J * P
    HS = 512
    HC = HS // P
    DC = D // P
    ROW = D + E
    EPS = 1e-5
    ROUTED_SCALE = 2.5
    BIG, LOW = 3.0e38, -3.0e38
    RING = 4

    BEFORE_EXPERTS = 3
    EARLY = 2
    FILL = 5, 3, 2, 2

    tok_rows = nc.dram_tensor("tok_rows", (TOKENS + P, ROW), fp32, kind="Internal").ap()

    ctx = ExitStack()
    with ctx:
        def sb(name, shape, dt=fp32):
            return ctx.enter_context(nc.sbuf_tensor(name, shape, dt))

        def sem(name):
            return ctx.enter_context(nc.semaphore(name))

        def wait(eng, semaphore, value):
            if not isinstance(value, int) or value > 0:
                eng.wait_ge(semaphore, value)

        def wait_apart(eng, semaphore, value):
            eng.wait_ge(semaphore, value)
            eng.sem_inc(waits_carried, 1)

        def span(first, end, step):
            return first, end - step + 1, step

        ident = sb("ident", [P, P])
        tri = sb("tri", [P, P], bf16)
        ones = sb("ones", [P, P], bf16)
        slot_col = sb("slot_col", [P, 1])
        slot_row = sb("slot_row", [P, P])
        restart = sb("restart", [P, E, TILES])
        one1 = sb("one1", [1, 1])
        minus_half = sb("minus_half", [P, J])
        zeros = sb("zeros", [P, ROW])
        biasb = sb("biasb", [P, E])
        gin = sb("gin", [P, 2])
        tg = sb("tg", [P, 2])
        wscale = sb("wscale", [P, 1])
        gwT = sb("gwT", [P, DC, E])
        suT = sb("suT", [P, DC, HS])
        sdT = sb("sdT", [P, HC, D])

        rows_all = sb("rows_all", [P, TILES, D])
        c4 = [sb(f"c4_{i}", [P, J, D]) for i in range(2)]
        ct4 = [sb(f"ct4_{i}", [P, J, DC, P]) for i in range(2)]
        q4 = [sb(f"q4_{i}", [P, 2, J, D]) for i in range(2)]
        sig_all = sb("sig_all", [P, 2, 2, DC, D])
        sig = [sig_all[:, i] for i in range(2)]
        rows = [sb(f"rows_{i}", [P, J, ROW]) for i in range(2)]
        xt4 = [sb(f"xt4_{i}", [P, DC, TG]) for i in range(2)]
        xt_all = sb("xt_all", [P, DC, TOKENS])
        stats1 = [sb(f"stats1_{i}", [P, J, 6]) for i in range(2)]
        mv1 = [sb(f"mv1_{i}", [P, J, 2]) for i in range(2)]
        ve1 = sb("ve1", [P, J])
        rstd1 = [sb(f"rstd1_{i}", [P, J]) for i in range(2)]
        neg1 = sb("neg1", [P, J])
        shift1 = [sb(f"shift1_{i}", [P, J]) for i in range(2)]
        stats2 = sb("stats2", [P, J, 6])
        mv2 = [sb(f"mv2_{i}", [P, J, 2]) for i in range(2)]
        ve2 = sb("ve2", [P, J])
        rstd2 = [sb(f"rstd2_{i}", [P, J]) for i in range(2)]
        scores = [sb(f"scores_{i}", [P, J, E]) for i in range(2)]
        biased = sb("biased", [P, J, E])
        pair_hi = sb("pair_hi", [P, J * G, 2])
        pair_lo = sb("pair_lo", [P, J * G, 2])
        top1 = sb("top1", [P, J * G])
        mid = sb("mid", [P, J * G])
        top2 = sb("top2", [P, J * G])
        group_in = sb("group_in", [P, J, G + K])
        group_top = sb("group_top", [P, J, 8])
        group_rep = sb("group_rep", [P, J, 8])
        group_out = sb("group_out", [P, J, G + K])
        group_sel = sb("group_sel", [P, J * G])
        masked = sb("masked", [P, J * G, EG])
        exp_in = sb("exp_in", [P, J, E + K])
        exp_top = sb("exp_top", [P, J, 8])
        exp_rep = sb("exp_rep", [P, J, 8])
        exp_out = sb("exp_out", [P, J, E + K])
        picked = sb("picked", [P, J, E])
        pick_sum = sb("pick_sum", [P, J])
        pick_inv = sb("pick_inv", [P, J])
        sel_all = sb("sel_all", [P, TILES, E], bf16)

        relu_h = [sb(f"relu_h_{i}", [P, TG]) for i in range(2)]
        hT = sb("hT", [P, HC, TG])
        upto = sb("upto", [P, E, TILES])
        before = sb("before", [P, E, TILES])
        before_n = sb("before_n", [P, E, TILES])
        upto_excl = sb("upto_excl", [1, E, TILES])
        tile_of = sb("tile_of", [P, E])
        base_of = sb("base_of", [P, E])
        rank = sb("rank", [P, E])
        bounds = sb("bounds", [P, 2, 8])
        from_lo = q4[0][:, 0, :, :].rearrange("p j (k q) -> p (j k) q", q=P)
        from_hi = q4[1][:, 0, :, :].rearrange("p j (k q) -> p (j k) q", q=P)
        onehot = sb("onehot", [P, 8, P], bf16)
        prefix = sb("prefix", [P, 8, P], bf16)
        cmp = sig_all[:, :, :, :, :].rearrange("p i b c (h q) -> p (i b c h) q", q=P)
        in_tile = sb("in_tile", [P, E])
        valid = sb("valid", [P, E])
        tok_a = sb("tok_a", [P, E])
        tok_b = sb("tok_b", [P, E])
        tok_c = sb("tok_c", [P, E])
        tok_id = sb("tok_id", [P, E], u32)
        slot_tok = sb("slot_tok", [P, 8], u32)
        wring = [sb(f"wring_{i}", [P, 2 * D]) for i in range(RING)]
        xe = [sb(f"xe_{i}", [P, ROW]) for i in range(RING)]
        xeT = [sb(f"xeT_{i}", [P, DC, P]) for i in range(2)]
        relu_e = sb("relu_e", [P, P])
        h_e = [sb(f"h_e_{i}", [P, P]) for i in range(2)]
        y_e = [sb(f"y_e_{i}", [P, D]) for i in range(2)]

        psum = ctx.enter_context(nc.psum_tensor("psum", [P, 8 * 512], fp32))
        bank = [psum[:, 512 * i:512 * i + 512] for i in range(8)]
        logits = [psum[:, 1024 * i:1024 * i + 1024] for i in range(2)]

        waits_carried = sem("waits_carried")
        params_loaded = sem("params_loaded")
        shared_loaded = sem("shared_loaded")
        dump_rows_zeroed = sem("dump_rows_zeroed")
        pool_self = sem("pool_self")
        norm1_self = sem("norm1_self")
        norm2_self = sem("norm2_self")
        index_copied = sem("index_copied")
        q_zeroed = sem("q_zeroed")
        consts_ready = sem("consts_ready")
        zeros_ready = sem("zeros_ready")
        marks_ready = sem("marks_ready")
        tanh_ready = sem("tanh_ready")
        x_loaded = [sem(f"x_loaded_{i}") for i in range(2)]
        ctx_loaded = [sem(f"ctx_loaded_{i}") for i in range(2)]
        stats1_ready = sem("stats1_ready")
        rstd1_ready = sem("rstd1_ready")
        q_ready = sem("q_ready")
        logits_ready = sem("logits_ready")
        sig_ready = sem("sig_ready")
        pv_ready = sem("pv_ready")
        x1_ready = sem("x1_ready")
        stats2_ready = sem("stats2_ready")
        rstd2_ready = sem("rstd2_ready")
        xn_ready = sem("xn_ready")
        xt_in_psum = sem("xt_in_psum")
        xt_ready = sem("xt_ready")
        gate_ready = sem("gate_ready")
        scores_ready = sem("scores_ready")
        routed = sem("routed")
        x1_stored = [sem(f"x1_stored_{i}") for i in range(2)]
        rows_stored = [sem(f"rows_stored_{i}") for i in range(2)]
        dve_self = sem("dve_self")
        totals_ready = sem("totals_ready")
        prefix_ready = sem("prefix_ready")
        scan_ready = sem("scan_ready")
        bounds_in_psum = sem("bounds_in_psum")
        onehot_ready = sem("onehot_ready")
        prefix_copied = sem("prefix_copied")
        counts_ready = sem("counts_ready")
        counts_read = sem("counts_read")
        table_ready = sem("table_ready")
        up_ready = sem("up_ready")
        relu_done = sem("relu_done")
        h_ready = sem("h_ready")
        y_ready = sem("y_ready")
        y_kept = sem("y_kept")
        weights_loaded = [sem(f"weights_loaded_{i}") for i in range(RING)]
        gathered = [sem(f"gathered_{i}") for i in range(RING)]
        xe_in_psum = sem("xe_in_psum")
        xeT_ready = sem("xeT_ready")
        he_in_psum = sem("he_in_psum")
        he_read = sem("he_read")
        he_ready = sem("he_ready")
        ye_in_psum = sem("ye_in_psum")
        ye_ready = sem("ye_ready")
        scattered = sem("scattered")
        shared_added = sem("shared_added")

        block = ctx.enter_context(nc.Block())

        tok_groups = tok_rows[0:TOKENS].rearrange("(g j p) d -> g p j d", j=J, p=P)
        out_groups = out[0:TOKENS].rearrange("(g j p) d -> g p j d", j=J, p=P)


        def nth(b, par):
            return b - par

        @block.sync
        def _(sp):
            def tiles(b):
                return rows_all[:, bass.ds(b * J, J), :]

            def load_x(b, par):
                sp.dma_start(tiles(b).rearrange("p j d -> p (j d)"), x[bass.ds(b, 1)].rearrange("g p f -> p (g f)")).then_inc(x_loaded[par], 16)

            def load_ctx_rows(b, par):
                sp.dma_start(c4[par][:, :, :].rearrange("p j d -> p (j d)"), ctx_rows[bass.ds(b, 1)].rearrange("g p f -> p (g f)")).then_inc(ctx_loaded[par], 16)

            def load_ctx_cols(b, par):
                sp.dma_start(ct4[par][:, :, :, :].rearrange("p j c d -> p (j c d)"), ctx_cols[bass.ds(b, 1)].rearrange("g p f -> p (g f)")).then_inc(ctx_loaded[par], 16)

            load_x(0, 0)
            sp.dma_start(gin[:, :], gates).then_inc(params_loaded, 16)
            load_ctx_rows(0, 0)
            load_ctx_cols(0, 0)
            sp.dma_start(biasb[:, :], bias).then_inc(params_loaded, 16)
            sp.dma_start(gwT[:, :, :].rearrange("p c e -> p (c e)"), gate_w).then_inc(params_loaded, 16)
            load_x(1, 1)
            load_ctx_rows(1, 1)
            load_ctx_cols(1, 1)
            sp.wait_ge(zeros_ready, 1)
            sp.dma_start(tok_rows[TOKENS:TOKENS + P], zeros[:, :]).then_inc(dump_rows_zeroed, 16)
            sp.dma_start(out[TOKENS:TOKENS + P], zeros[:, 0:D]).then_inc(dump_rows_zeroed, 16)
            sp.dma_start(suT[:, :, :].rearrange("p c e -> p (c e)"), shared_up).then_inc(shared_loaded, 16)
            sp.dma_start(sdT[:, :, :].rearrange("p c e -> p (c e)"), shared_down).then_inc(shared_loaded, 16)

            def store_x1(b, par):
                sp.wait_ge(x1_ready, J * b + J)
                sp.dma_start(out_groups[bass.ds(b, 1)].rearrange("g p j d -> p (g j) d"), tiles(b)).then_inc(x1_stored[par], 16)

            def store_rows(b, par):
                sp.wait_ge(routed, b + 1)
                sp.dma_start(tok_groups[bass.ds(b, 1)].rearrange("g p j d -> p (g j) d"), rows[par][:, :, :]).then_inc(rows_stored[par], 16)

            def step(s, h, live):
                now, prev, prev2 = live
                if now and (not isinstance(s, int) or s + 2 < GROUPS):
                    sp.wait_ge(stats1_ready, s + 1)
                    load_x(s + 2, h)
                if prev:
                    if not isinstance(s, int) or s + 1 < GROUPS:
                        sp.wait_ge(logits_ready, J * s)
                        load_ctx_rows(s + 1, 1 - h)
                        sp.wait_ge(pv_ready, J * s)
                        load_ctx_cols(s + 1, 1 - h)
                    store_x1(s - 1, 1 - h)
                if prev2:
                    store_rows(s - 2, h)

            step(0, 0, (True, False, False))
            step(1, 1, (True, True, False))
            with sp.Fori(*span(2, GROUPS - 2, 2)) as s:
                for h in range(2):
                    step(s + h, h, (True, True, True))
            step(GROUPS - 2, 0, (True, True, True))
            step(GROUPS - 1, 1, (True, True, True))
            step(GROUPS, 0, (False, True, True))
            step(GROUPS + 1, 1, (False, False, True))

            def load_weights(e, r):
                sp.dma_start(wring[r][:, :], expert_w[bass.ds(e, 1)].rearrange("e p f -> p (e f)")).then_inc(weights_loaded[r], 16)

            for r in range(RING):
                load_weights(r, r)
            with sp.Fori(*span(0, E - RING, RING)) as e0:
                for r in range(RING):
                    sp.wait_ge(ye_in_psum, e0 + r + 1)
                    load_weights(e0 + r + RING, r)

        @block.gpsimd
        def _(pool):
            pool.memset(zeros[:, :], 0.0).then_inc(zeros_ready, 1)
            pool.memset(ident[:, :], 0.0).then_inc(pool_self, 1)
            pool.memset(minus_half[:, :], -0.5).then_inc(pool_self, 1)
            pool.wait_ge(pool_self, 2)
            pool.affine_select(out=ident[:, :], in_=ident[:, :], compare_op=ALU.not_equal, fill=1.0, base=0,
                               pattern=[[-1, P]], channel_multiplier=1).then_inc(consts_ready, 1)
            pool.memset(ones[:, :], 1.0).then_inc(consts_ready, 1)
            pool.memset(one1[:, :], 1.0).then_inc(consts_ready, 1)
            pool.wait_ge(consts_ready, 2)
            pool.affine_select(out=tri[:, :], in_=ones[:, :], compare_op=ALU.is_ge, fill=0.0, base=0,
                               pattern=[[1, P]], channel_multiplier=-1).then_inc(consts_ready, 1)
            pool.iota(slot_col[:, :], pattern=[[0, 1]], base=0, channel_multiplier=1,
                      allow_small_or_imprecise_dtypes=True).then_inc(consts_ready, 1)
            pool.iota(slot_row[:, :], pattern=[[1, P]], base=0, channel_multiplier=0,
                      allow_small_or_imprecise_dtypes=True).then_inc(consts_ready, 1)

            def norm1(b, par):
                wait_apart(pool, stats1_ready, b + 1)
                pool.tensor_scalar(ve1[:, :], mv1[par][:, :, 1], EPS, None, op0=ALU.add).then_inc(norm1_self, 1)
                pool.tensor_scalar(neg1[:, :], mv1[par][:, :, 0], -1.0, None, op0=ALU.mult).then_inc(norm1_self, 1)
                pool.wait_ge(norm1_self, 3 * b + 2)
                pool.tensor_tensor(rstd1[par][:, :], ve1[:, :], minus_half[:, :], ALU.pow).then_inc(norm1_self, 1)
                pool.wait_ge(norm1_self, 3 * b + 3)
                pool.tensor_tensor(shift1[par][:, :], neg1[:, :], rstd1[par][:, :], ALU.mult).then_inc(rstd1_ready, 1)

            def norm2(b, par):
                wait_apart(pool, stats2_ready, b + 1)
                pool.tensor_scalar(ve2[:, :], mv2[par][:, :, 1], EPS, None, op0=ALU.add).then_inc(norm2_self, 1)
                pool.wait_ge(norm2_self, b + 1)
                pool.tensor_tensor(rstd2[par][:, :], ve2[:, :], minus_half[:, :], ALU.pow).then_inc(rstd2_ready, 1)

            norm1(0, 0)
            pool.memset(restart[:, :, :], 1.0).then_inc(consts_ready, 1)
            pool.wait_ge(consts_ready, 7)
            pool.memset(restart[:, :, 0:1], 0.0).then_inc(consts_ready, 1)
            with pool.Fori(*span(0, GROUPS - 2, 2)) as b:
                for h in range(2):
                    norm1(b + h + 1, 1 - h)
                    norm2(b + h, h)
            norm1(GROUPS - 1, 1)
            norm2(GROUPS - 2, 0)
            norm2(GROUPS - 1, 1)


            def gather(e, r):
                pool.tensor_copy(slot_tok[:, r % 8:r % 8 + 1], tok_id[:, bass.ds(e, 1)]).then_inc(index_copied, 1)
                wait_apart(pool, index_copied, e + 1)
                pool.indirect_dma_start(xe[r % RING][:, :], None, tok_rows,
                                        bass.IndirectOffsetOnAxis(ap=slot_tok[:, r % 8:r % 8 + 1], axis=0)).then_inc(gathered[r % RING], 16)

            def scatter(e, r):
                wait_apart(pool, ye_ready, e + 1)
                pool.indirect_dma_start(out, bass.IndirectOffsetOnAxis(ap=slot_tok[:, r % 8:r % 8 + 1], axis=0),
                                        y_e[r % 2][:, :], None, compute_op=ALU.add).then_inc(scattered, 16)

            pool.wait_ge(table_ready, 1)
            pool.wait_ge(dump_rows_zeroed, 32)
            for par in range(2):
                pool.wait_ge(rows_stored[par], 16 * GROUPS // 2)
                pool.wait_ge(x1_stored[par], 16 * GROUPS // 2)
            for r in range(RING):
                gather(r, r)

            def add_shared(n):
                wait(pool, y_kept, J * n + J)
                pool.dma_start(out_groups[n], rows_all[:, n * J:n * J + J, :], accum_op=ALU.add).then_inc(shared_added, 16)

            for n in range(EARLY):
                add_shared(n)
            pool.wait_ge(shared_added, 16 * EARLY)

            def slots(e0, last_):
                for r in range(8):
                    scatter(e0 + r, r)
                    if not (last_ and r >= 8 - RING):
                        gather(e0 + r + RING, r + RING)
                    wait_apart(pool, scattered, 16 * e0 + 16 * (r + 1))

            with pool.Fori(*span(0, E - 8, 8)) as e0:
                slots(e0, False)
            slots(E - 8, True)
            for n in range(EARLY, GROUPS):
                add_shared(n)
            pool.wait_ge(shared_added, 16 * GROUPS)

        @block.scalar
        def _(act):
            act.wait_ge(params_loaded, 48)
            nc.scalar.activation(tg[:, :], gin[:, :], ACT.Tanh).then_inc(tanh_ready, 1)

            def normed_queries(b, par, j):
                if j == 0:
                    act.wait_ge(rstd1_ready, b + 1)
                for k in range(2):
                    own_rows = slice(S * k, S * k + S)
                    last = nc.scalar.activation(q4[par][own_rows, k, j, :], rows_all[own_rows, bass.ds(b * J + j, 1), :].rearrange("p t d -> p (t d)"),
                                                ACT.Identity, bias=shift1[par][own_rows, j:j + 1], scale=rstd1[par][own_rows, j:j + 1])
                last.then_inc(q_ready, 1)

            def sigmoid(s, j):
                t = s * J + j
                act.wait_ge(logits_ready, t + 1)
                wait(act, pv_ready, t - 1)
                nc.scalar.activation(sig[j % 2][:, :, :, :].rearrange("p b c m -> p (b c m)"), logits[j % 2], ACT.Sigmoid,
                                     scale=float(S) ** -0.5).then_inc(sig_ready, 1)

            def copy_xt(b, par, dc):
                act.wait_ge(xt_in_psum, 2 * b + dc + 1)
                nc.scalar.copy(xt4[par][:, dc, :], bank[6][:, :])
                nc.scalar.copy(xt_all[:, dc, bass.ds(b * TG, TG)], bank[6][:, :]).then_inc(xt_ready, 1)

            def score(b, par):
                act.wait_ge(gate_ready, b + 1)
                nc.scalar.activation(scores[par][:, :, :].rearrange("p j e -> p (j e)"), bank[7][:, 0:J * E],
                                     ACT.Sigmoid).then_inc(scores_ready, 1)

            def step(s, h, live):
                now, prev, prev2 = live
                more = now and (not isinstance(s, int) or s + 1 < GROUPS)
                if now:
                    sigmoid(s, 0)
                if prev2:
                    score(s - 2, h)
                if now:
                    sigmoid(s, 1)
                if more:
                    normed_queries(s + 1, 1 - h, 0)
                    normed_queries(s + 1, 1 - h, 1)
                if now:
                    sigmoid(s, 2)
                if prev:
                    copy_xt(s - 1, 1 - h, 0)
                if more:
                    normed_queries(s + 1, 1 - h, 2)
                    normed_queries(s + 1, 1 - h, 3)
                if now:
                    sigmoid(s, 3)
                if prev:
                    copy_xt(s - 1, 1 - h, 1)

            def up_chunk(n, c):
                u = HC * n + c
                act.wait_ge(up_ready, u + 1)
                nc.scalar.activation(relu_h[c % 2][:, :], bank[c % 2][:, :], ACT.Relu).then_inc(relu_done, 1)
                act.wait_ge(relu_done, u + 1)
                nc.scalar.activation(hT[:, c, :], relu_h[c % 2][:, :], ACT.Square).then_inc(h_ready, 1)

            def down_tile(n, j):
                t = J * n + j
                act.wait_ge(y_ready, t + 1)
                nc.scalar.activation(rows_all[:, bass.ds(t, 1), :].rearrange("p t d -> p (t d)"), bank[2 + j % 2][:, 0:D],
                                     ACT.Copy, scale=tg[:, 1:2]).then_inc(y_kept, 1)

            for j in range(J):
                normed_queries(0, 0, j)
            step(0, 0, (True, False, False))
            step(1, 1, (True, True, False))
            with act.Fori(*span(2, GROUPS - 2, 2)) as s:
                for h in range(2):
                    step(s + h, h, (True, True, True))
            step(GROUPS - 2, 0, (True, True, True))
            step(GROUPS - 1, 1, (True, True, True))
            score(GROUPS - 2, 0)
            up_chunk(0, 0)
            copy_xt(GROUPS - 1, 1, 0)
            copy_xt(GROUPS - 1, 1, 1)
            up_chunk(0, 1)
            score(GROUPS - 1, 1)

            for c in range(2, HC):
                up_chunk(0, c)
            for par in range(2):
                act.wait_ge(x1_stored[par], 16 * GROUPS // 2)
            for j in range(J):
                down_tile(0, j)
            with act.Fori(1, GROUPS) as n:
                for c in range(HC):
                    up_chunk(n, c)
                for j in range(J):
                    down_tile(n, j)

        @block.tensor
        def _(pe):
            pe.wait_ge(consts_ready, 6)

            def qk(s, h, j):
                t = s * J + j
                if j == 0:
                    pe.wait_ge(ctx_loaded[h], 16 * nth(s, h) + 32)
                pe.wait_ge(q_ready, t + 1)
                wait(pe, sig_ready, t - 1)
                for half in range(DC):
                    for b in range(2):
                        last = nc.tensor.matmul(bank[2 * (j % 2) + b][:, half * D:half * D + D],
                                                q4[h][:, b, j, half * P:half * P + P], c4[h][:, j, :],
                                                start=True, stop=True)
                last.then_inc(logits_ready, 1)

            def pv(s, h, j):
                t = s * J + j
                pe.wait_ge(sig_ready, t + 1)
                wait(pe, x1_ready, t - 1)
                for half in range(DC):
                    for b in range(2):
                        last = nc.tensor.matmul(bank[4 + j % 2][S * b:S * b + S, 0:D],
                                                ct4[h][:, j, half, S * b:S * b + S], sig[j % 2][:, b, half, :],
                                                start=(half == 0), stop=(half == DC - 1))
                last.then_inc(pv_ready, 1)

            def transpose_rows(b, par, dc):
                pe.wait_ge(xn_ready, b + 1)
                wait(pe, xt_ready, 2 * b + dc)
                for j in range(J):
                    last = nc.tensor.transpose(bank[6][:, j * P:j * P + P], rows[par][:, j, dc * P:dc * P + P], ident[:, :])
                last.then_inc(xt_in_psum, 1)

            def gate(b, par):
                pe.wait_ge(xt_ready, 2 * b + 2)
                for j in range(J):
                    for dc in range(DC):
                        last = nc.tensor.matmul(bank[7][:, j * E:j * E + E], xt4[par][:, dc, j * P:j * P + P],
                                                gwT[:, dc, :], start=(dc == 0), stop=(dc == DC - 1))
                last.then_inc(gate_ready, 1)

            def step(s, h, live):
                now, prev, prev2 = live
                if now:
                    qk(s, h, 0)
                if prev:
                    pv(s - 1, 1 - h, J - 1)
                if prev2:
                    gate(s - 2, h)
                if now:
                    qk(s, h, 1)
                    pv(s, h, 0)
                    qk(s, h, 2)
                    pv(s, h, 1)
                if prev:
                    transpose_rows(s - 1, 1 - h, 0)
                if now:
                    qk(s, h, 3)
                    pv(s, h, 2)
                if prev:
                    transpose_rows(s - 1, 1 - h, 1)

            def totals():
                pe.wait_ge(routed, GROUPS)
                pe.wait_ge(pv_ready, TILES)
                for half in range(2):
                    lo = half * (TILES // 2)
                    last = nc.tensor.matmul(bank[4 + half][:, :], ones[:, :],
                                            sel_all[:, lo:lo + TILES // 2, :].rearrange("p i e -> p (i e)"), start=True, stop=True)
                last.then_inc(totals_ready, 1)
                pe.wait_ge(xt_ready, 2 * GROUPS)
                for k in range(8):
                    for q in range(4):
                        last = nc.tensor.matmul(bank[6 + k // 4][32 * q:32 * q + 32, (k % 4) * P:(k % 4) * P + P],
                                                sel_all[:, :, 4 * k + q], tri[:, :], start=True, stop=True,
                                                tile_position=(0, 32 * q))
                last.then_inc(prefix_ready, 1)

            def bounds_up():
                pe.wait_ge(scan_ready, 1)
                for hi in range(2):
                    for k in range(8):
                        row = (upto if hi else upto_excl)[0:1, 4 * k:4 * k + 4, :].rearrange("p e i -> p (e i)")
                        last = nc.tensor.matmul(bank[4][:, hi * 8 + k:hi * 8 + k + 1], row, one1[0:1, 0:1], start=True, stop=True)
                last.then_inc(bounds_in_psum, 1)

            def counts(r):
                if r == 0:
                    pe.wait_ge(onehot_ready, 1)
                    pe.wait_ge(prefix_copied, 1)
                else:
                    pe.wait_ge(counts_read, 1)
                for q in range(4):
                    for k in range(4):
                        kk = 4 * r + k
                        last = nc.tensor.matmul(bank[4 + q][:, k * P:k * P + P], onehot[32 * q:32 * q + 32, kk, :],
                                                prefix[32 * q:32 * q + 32, kk, :], start=True, stop=True,
                                                tile_position=(32 * q, 0))
                last.then_inc(counts_ready, 1)

            def up_chunk(n, c):
                u = HC * n + c
                wait(pe, h_ready, u - 1)
                for dc in range(DC):
                    last = nc.tensor.matmul(bank[c % 2][:, :], suT[:, dc, c * P:c * P + P],
                                            xt_all[:, dc, bass.ds(n * TG, TG)], start=(dc == 0), stop=(dc == DC - 1))
                last.then_inc(up_ready, 1)

            def down_tile(n, j):
                t = J * n + j
                pe.wait_ge(h_ready, HC * n + HC)
                wait(pe, y_kept, t - 1)
                for c in range(HC):
                    last = nc.tensor.matmul(bank[2 + j % 2][:, 0:D], hT[:, c, j * P:j * P + P], sdT[:, c, :],
                                            start=(c == 0), stop=(c == HC - 1))
                last.then_inc(y_ready, 1)

            def shared_piece(n, k):
                up_chunk(n, k) if k < HC else down_tile(n, k - HC)

            def rows_T(e, r):
                pe.wait_ge(gathered[r % RING], 16 * ((e - r % RING) // RING) + 16 if isinstance(e, int) else 4 * (e - r % RING) + 16)
                wait(pe, xeT_ready, e)
                for dc in range(DC):
                    last = nc.tensor.transpose(bank[4][:, dc * P:dc * P + P], xe[r % RING][:, dc * P:dc * P + P], ident[:, :])
                last.then_inc(xe_in_psum, 1)

            def expert_up(e, r):
                pe.wait_ge(weights_loaded[r % RING], 16 * ((e - r % RING) // RING) + 16 if isinstance(e, int) else 4 * (e - r % RING) + 16)
                pe.wait_ge(xeT_ready, e + 1)
                wait(pe, he_ready, e)
                for dc in range(DC):
                    last = nc.tensor.matmul(bank[5][:, 0:P], wring[r % RING][:, dc * P:dc * P + P], xeT[r % 2][:, dc, :],
                                            start=(dc == 0), stop=(dc == DC - 1))
                last.then_inc(he_in_psum, 1)

            def expert_down(e, r):
                pe.wait_ge(he_ready, e + 1)
                wait(pe, ye_ready, e)
                nc.tensor.matmul(bank[6][:, 0:D], h_e[r % 2][:, :], wring[r % RING][:, D:2 * D],
                                 start=True, stop=True).then_inc(ye_in_psum, 1)

            pe.wait_ge(params_loaded, 48)
            pe.wait_ge(q_zeroed, 4)
            step(0, 0, (True, False, False))
            step(1, 1, (True, True, False))
            with pe.Fori(*span(2, GROUPS, 2)) as s:
                for h in range(2):
                    step(s + h, h, (True, True, True))

            pieces = [(n, k) for n in range(BEFORE_EXPERTS) for k in range(8)]

            def fill(count):
                for _ in range(count):
                    shared_piece(*pieces.pop(0))

            pe.wait_ge(shared_loaded, 32)
            pv(GROUPS - 1, 1, J - 1)
            gate(GROUPS - 2, 0)
            pe.wait_ge(sig_ready, TILES)
            fill(1)
            transpose_rows(GROUPS - 1, 1, 0)
            transpose_rows(GROUPS - 1, 1, 1)
            fill(1)
            gate(GROUPS - 1, 1)
            fill(FILL[0])
            totals()
            fill(FILL[1])
            bounds_up()
            fill(FILL[2])
            counts(0)
            fill(FILL[3])
            counts(1)
            fill(len(pieces))

            rows_T(0, 0)

            def slots(n, e0, first, last_):
                for k in range(8):
                    e = e0 + k
                    expert_up(e, k)
                    if not (last_ and k == 7):
                        rows_T(e + 1, k + 1)
                    if not (first and k == 0):
                        expert_down(e - 1, k + 7)
                    shared_piece(n, k)

            slots(BEFORE_EXPERTS, 0, True, False)
            with pe.Fori(BEFORE_EXPERTS + 1, BEFORE_EXPERTS + 3) as n:
                slots(n, n * 8 - BEFORE_EXPERTS * 8, False, False)
            slots(BEFORE_EXPERTS + 3, E - 8, False, True)
            expert_down(E - 1, 7)
            with pe.Fori(BEFORE_EXPERTS + 4, GROUPS) as n:
                for k in range(8):
                    shared_piece(n, k)

        @block.vector
        def _(dve):
            V = nc.vector

            class Own:
                def __init__(self):
                    self.base, self.n = 0, 0

                def mark(self, instruction):
                    instruction.then_inc(dve_self, 1)
                    self.n += 1

                def wait(self):
                    dve.wait_ge(dve_self, self.base + self.n)

                def wait_apart(self):
                    wait_apart(dve, dve_self, self.base + self.n)

            own = Own()

            for par in range(2):
                for k in range(2):
                    other = slice(S * (1 - k), S * (1 - k) + S)
                    V.memset(q4[par][other, k, :, :], 0.0).then_inc(q_zeroed, 1)
            own.mark(V.memset(group_in[:, :, :], LOW))
            own.mark(V.memset(group_rep[:, :, :], LOW))
            own.mark(V.memset(exp_in[:, :, :], LOW))
            own.mark(V.memset(exp_rep[:, :, :], LOW))

            def tile(t, part=slice(0, P)):
                return rows_all[part, bass.ds(t, 1), :].rearrange("p t d -> p (t d)")

            def norm1_stats(b, par):
                wait_apart(dve, x_loaded[par], 8 * nth(b, par) + 16)
                for j in range(J):
                    own.mark(V.bn_stats(stats1[par][:, j, :], tile(b * J + j)))
                own.wait_apart()
                for j in range(J):
                    last = V.bn_aggr(mv1[par][:, j, :], stats1[par][:, j, :])
                last.then_inc(stats1_ready, 1)

            def residual(s, h, j):
                t = s * J + j
                dve.wait_ge(pv_ready, t + 1)
                V.scalar_tensor_tensor(tile(t), bank[4 + j % 2][:, 0:D], tg[:, 0:1], tile(t),
                                       op0=ALU.mult, op1=ALU.add).then_inc(x1_ready, 1)
                wait_apart(dve, x1_ready, t + 1)
                own.mark(V.bn_stats(stats2[:, j, :], tile(t)))
                if j == J - 1:
                    own.wait_apart()
                    for k in range(J):
                        last = V.bn_aggr(mv2[h][:, k, :], stats2[:, k, :])
                    last.then_inc(stats2_ready, 1)

            def norm2_apply(b, par):
                dve.wait_ge(rstd2_ready, b + 1)
                if not isinstance(b, int) or b >= 2:
                    dve.wait_ge(rows_stored[par], 8 * nth(b, par))
                    dve.wait_ge(xt_in_psum, 2 * b - 2)
                for j in range(J):
                    last = V.tensor_scalar(rows[par][:, j, 0:D], tile(b * J + j), mv2[par][:, j, 0:1], rstd2[par][:, j:j + 1],
                                           op0=ALU.subtract, op1=ALU.mult)
                last.then_inc(xn_ready, 1)

            def do(instruction):
                own.mark(instruction)
                own.wait()

            def route_groups(b, par):
                dve.wait_ge(scores_ready, b + 1)
                sc = scores[par]
                do(V.tensor_tensor(biased[:, :, :], sc[:, :, :], biasb[:, :].unsqueeze(1).to_broadcast([P, J, E]), ALU.add))
                bv = biased[:, :, :].rearrange("p j (g a b) -> p (j g) a b", g=G, a=2)
                own.mark(V.tensor_tensor(pair_hi[:, :, :], bv[:, :, :, 0], bv[:, :, :, 1], ALU.max))
                do(V.tensor_tensor(pair_lo[:, :, :], bv[:, :, :, 0], bv[:, :, :, 1], ALU.min))
                own.mark(V.tensor_tensor(top1[:, :], pair_hi[:, :, 0], pair_hi[:, :, 1], ALU.max))
                own.mark(V.tensor_tensor(mid[:, :], pair_hi[:, :, 0], pair_hi[:, :, 1], ALU.min))
                do(V.tensor_tensor(top2[:, :], pair_lo[:, :, 0], pair_lo[:, :, 1], ALU.max))
                do(V.tensor_tensor(mid[:, :], mid[:, :], top2[:, :], ALU.max))
                own.mark(V.tensor_tensor(group_in[:, :, 0:G], top1[:, :].rearrange("p (j g) -> p j g", g=G),
                                         mid[:, :].rearrange("p (j g) -> p j g", g=G), ALU.add))

            def route_masks(b, par):
                own.wait_apart()
                for j in range(J):
                    own.mark(V.max(group_top[:, j, :], group_in[:, j, 0:G]))
                own.wait()
                own.mark(V.tensor_copy(group_rep[:, :, 0:K], group_top[:, :, 0:K]))
                own.wait_apart()
                for j in range(J):
                    own.mark(V.match_replace(group_out[:, j, :], group_rep[:, j, :], group_in[:, j, :], BIG))
                own.wait()
                do(V.tensor_scalar(group_sel[:, :].rearrange("p (j g) -> p j g", g=G), group_out[:, :, 0:G], BIG / 2, None, op0=ALU.is_ge))
                do(V.tensor_tensor(masked[:, :, :], biased[:, :, :].rearrange("p j (g a) -> p (j g) a", g=G),
                                   group_sel[:, :].unsqueeze(2).to_broadcast([P, J * G, EG]), ALU.mult))
                own.mark(V.tensor_scalar(exp_in[:, :, 0:E], masked[:, :, :].rearrange("p (j g) a -> p j (g a)", j=J), 0.0, None, op0=ALU.add))

            def route_experts(b, par):
                sc = scores[par]
                own.wait_apart()
                for j in range(J):
                    own.mark(V.max(exp_top[:, j, :], exp_in[:, j, 0:E]))
                own.wait()
                own.mark(V.tensor_copy(exp_rep[:, :, 0:K], exp_top[:, :, 0:K]))
                own.wait_apart()
                for j in range(J):
                    own.mark(V.match_replace(exp_out[:, j, :], exp_rep[:, j, :], exp_in[:, j, :], BIG))
                own.wait()
                own.mark(V.tensor_scalar(sel_all[:, bass.ds(b * J, J), :], exp_out[:, :, 0:E], BIG / 2, None, op0=ALU.is_ge))
                do(V.scalar_tensor_tensor(picked[:, :, :], exp_out[:, :, 0:E], BIG / 2, sc[:, :, :], op0=ALU.is_ge, op1=ALU.mult))
                do(V.tensor_reduce(pick_sum[:, :], picked[:, :, :], AX.X, ALU.add))
                do(V.tensor_scalar(pick_sum[:, :], pick_sum[:, :], 1e-20, None, op0=ALU.add))
                do(V.reciprocal(pick_inv[:, :], pick_sum[:, :]))
                do(V.tensor_scalar(pick_inv[:, :], pick_inv[:, :], wscale[:, 0:1], None, op0=ALU.mult))
                V.tensor_tensor(rows[par][:, :, D:ROW], picked[:, :, :], pick_inv[:, :].unsqueeze(2).to_broadcast([P, J, E]),
                                ALU.mult).then_inc(routed, 1)

            def step(s, h, live):
                now, prev, prev2 = live
                more = now and (not isinstance(s, int) or s + 1 < GROUPS)
                if prev:
                    residual(s - 1, 1 - h, J - 1)
                if more:
                    norm1_stats(s + 1, 1 - h)
                if prev2:
                    route_groups(s - 2, h)
                if prev:
                    norm2_apply(s - 1, 1 - h)
                if now:
                    residual(s, h, 0)
                if prev2:
                    route_masks(s - 2, h)
                if now:
                    residual(s, h, 1)
                if now:
                    residual(s, h, 2)
                if prev2:
                    route_experts(s - 2, h)

            norm1_stats(0, 0)
            dve.wait_ge(tanh_ready, 1)
            own.mark(V.tensor_scalar(wscale[:, :], tg[:, 1:2], ROUTED_SCALE, None, op0=ALU.mult))
            step(0, 0, (True, False, False))
            step(1, 1, (True, True, False))
            PER_STEP = 43
            start = own.n
            with dve.Fori(*span(2, GROUPS - 2, 2)) as s:
                own.base, own.n = (s - 2) * PER_STEP + start, 0
                for h in range(2):
                    step(s + h, h, (True, True, True))
                assert own.n == 2 * PER_STEP, own.n
            own.base, own.n = 0, start + (GROUPS - 4) * PER_STEP
            step(GROUPS - 2, 0, (True, True, True))
            step(GROUPS - 1, 1, (True, True, True))
            residual(GROUPS - 1, 1, J - 1)
            norm2_apply(GROUPS - 1, 1)
            for b in range(GROUPS - 2, GROUPS):
                route_groups(b, b % 2)
                route_masks(b, b % 2)
                route_experts(b, b % 2)

            dve.wait_ge(consts_ready, 8)
            dve.wait_ge(totals_ready, 1)
            for half in range(2):
                i0 = half * (TILES // 2)
                own.mark(V.tensor_copy(before_n[:, :, i0:i0 + TILES // 2],
                                       bank[4 + half][:, :].rearrange("p (i e) -> p e i", e=E)))
            own.wait()
            own.mark(V.tensor_tensor_scan(upto[:, :, :].rearrange("p e i -> p (e i)"), restart[:, :, :].rearrange("p e i -> p (e i)"),
                                          before_n[:, :, :].rearrange("p e i -> p (e i)"), 0.0, ALU.mult, ALU.add))
            own.wait()
            V.tensor_tensor(upto_excl[0:1, :, :], upto[0:1, :, :], before_n[0:1, :, :], ALU.subtract).then_inc(scan_ready, 1)
            dve.wait_ge(scan_ready, 1)
            tot = upto[:, :, :]
            do(V.tensor_scalar(before[:, :, :], tot, slot_col[:, 0:1], None, op0=ALU.is_le))
            dve.wait_ge(prefix_ready, 1)
            for half in range(2):
                last = V.tensor_copy(prefix[:, 4 * half:4 * half + 4, :].rearrange("p k q -> p (k q)"), bank[6 + half][:, :])
            last.then_inc(prefix_copied, 1)
            dve.wait_ge(bounds_in_psum, 1)
            do(V.tensor_copy(bounds[:, :, :].rearrange("p h k -> p (h k)"), bank[4][:, 0:16]))
            slotb = slot_row[:, :].unsqueeze(1).to_broadcast([P, 8, P])
            own.mark(V.tensor_tensor(from_lo[:, :, :], slotb, bounds[:, 0, :].unsqueeze(2).to_broadcast([P, 8, P]), ALU.is_ge))
            do(V.tensor_tensor(from_hi[:, :, :], slotb, bounds[:, 1, :].unsqueeze(2).to_broadcast([P, 8, P]), ALU.is_ge))
            V.tensor_tensor(onehot[:, :, :], from_lo[:, :, :], from_hi[:, :, :], ALU.subtract).then_inc(onehot_ready, 1)
            own.mark(V.tensor_reduce(tile_of[:, :], before[:, :, :], AX.X, ALU.add))
            do(V.tensor_tensor(before_n[:, :, :], before[:, :, :], tot, ALU.mult))
            do(V.tensor_reduce(base_of[:, :], before_n[:, :, :], AX.X, ALU.max))
            do(V.tensor_scalar(rank[:, :], base_of[:, :], -1.0, slot_col[:, 0:1], op0=ALU.mult, op1=ALU.add))
            for r in range(2):
                dve.wait_ge(counts_ready, r + 1)
                for q in range(4):
                    e0 = 16 * r + q
                    last = V.tensor_tensor(cmp[:, 4 * q:4 * q + 4, :], bank[4 + q][:, :].rearrange("p (k q) -> p k q", q=P),
                                           rank[:, e0:e0 + 13:4].unsqueeze(2).to_broadcast([P, 4, P]), ALU.is_le)
                    own.mark(last)
                own.wait()
                last = V.tensor_reduce(in_tile[:, 16 * r:16 * r + 16].rearrange("p (k q) -> p q k", q=4),
                                       cmp[:, :, :].rearrange("p (q k) t -> p q k t", q=4), AX.X, ALU.add)
                last.then_inc(counts_read, 1)
            dve.wait_ge(counts_read, 2)
            do(V.tensor_scalar(valid[:, :], tile_of[:, :], float(TILES), None, op0=ALU.is_lt))
            own.mark(V.tensor_tensor(tok_a[:, :], in_tile[:, :], valid[:, :], ALU.mult))
            do(V.tensor_scalar(tok_b[:, :], valid[:, :], -1.0, 1.0, op0=ALU.mult, op1=ALU.add))
            do(V.tensor_scalar(tok_c[:, :], tok_b[:, :], slot_col[:, 0:1], None, op0=ALU.mult))
            do(V.scalar_tensor_tensor(tok_b[:, :], tile_of[:, :], float(P), tok_a[:, :], op0=ALU.mult, op1=ALU.add))
            V.tensor_tensor(tok_id[:, :], tok_b[:, :], tok_c[:, :], ALU.add).then_inc(table_ready, 1)

            def copy_rows_T(e, r):
                dve.wait_ge(xe_in_psum, e + 1)
                wait(dve, he_in_psum, e - 1)
                V.tensor_copy(xeT[r % 2][:, :, :].rearrange("p c s -> p (c s)"), bank[4][:, 0:D]).then_inc(xeT_ready, 1)

            def hidden(e, r):
                dve.wait_ge(he_in_psum, e + 1)
                V.tensor_scalar(relu_e[:, :], bank[5][:, 0:P], 0.0, None, op0=ALU.max).then_inc(he_read, 1)
                dve.wait_ge(he_read, e + 1)
                wait(dve, ye_in_psum, e - 1)
                V.tensor_tensor(h_e[r % 2][:, :], relu_e[:, :], relu_e[:, :], ALU.mult).then_inc(he_ready, 1)

            def weigh(e, r):
                dve.wait_ge(ye_in_psum, e + 1)
                wait(dve, scattered, 16 * (e - 1))
                V.tensor_scalar(y_e[r % 2][:, :], bank[6][:, 0:D], xe[r % RING][:, bass.ds(e + D, 1)], None,
                                op0=ALU.mult).then_inc(ye_ready, 1)

            def slots(e0, first, last_):
                for k in range(8):
                    e = e0 + k
                    hidden(e, k)
                    if not (last_ and k == 7):
                        copy_rows_T(e + 1, k + 1)
                    if not (first and k == 0):
                        weigh(e - 1, k + 7)

            copy_rows_T(0, 0)
            slots(0, True, False)
            with dve.Fori(*span(8, E - 8, 8)) as e0:
                slots(e0, False, False)
            slots(E - 8, False, True)
            weigh(E - 1, 7)


_INS = ("x", "ctx_rows", "ctx_cols", "gates", "gate_w", "bias", "shared_up", "shared_down", "expert_w")


def kernel(x, ctx_2048, g_xattn, g_ffn, L0_ffn_gate_w, L0_ffn_bias_corr, L0_ffn_up_w, L0_ffn_down_w,
           L0_ffn_shared_up_w, L0_ffn_shared_down_w):
    import concourse.bacc as bacc
    from concourse.bass_utils import run_bass_kernel_spmd

    arr = lambda a: np.ascontiguousarray(np.asarray(a))
    x, c = np.asarray(x), np.asarray(ctx_2048)
    B, S, D = x.shape
    E, H, _ = L0_ffn_up_w.shape

    def groups(a):
        return arr(a.reshape(-1, 4, 128, D).transpose(0, 2, 1, 3).reshape(-1, 128, 4 * D))

    def cols(w):
        w = np.asarray(w)
        return arr(w.T.reshape(-1, 128, w.shape[0]).transpose(1, 0, 2).reshape(128, -1))

    ct = arr(c.reshape(-1, 4, 2, S, 2, 128).transpose(0, 5, 1, 4, 2, 3).reshape(-1, 128, 4 * 2 * 128))
    up = np.asarray(L0_ffn_up_w).transpose(0, 2, 1).reshape(E, 2, 128, H).transpose(0, 2, 1, 3).reshape(E, 128, 2 * H)
    down = np.asarray(L0_ffn_down_w).transpose(0, 2, 1)
    arrays = {
        "x": groups(x),
        "ctx_rows": groups(c),
        "ctx_cols": ct,
        "gates": arr(np.broadcast_to(np.stack([np.asarray(g_xattn)[0], np.asarray(g_ffn)[0]]), (128, 2))),
        "gate_w": cols(L0_ffn_gate_w),
        "bias": arr(np.broadcast_to(np.asarray(L0_ffn_bias_corr), (128, E))),
        "shared_up": cols(L0_ffn_shared_up_w),
        "shared_down": cols(L0_ffn_shared_down_w),
        "expert_w": arr(np.concatenate([up, down], axis=2)),
    }
    nc = bacc.Bacc("TRN2", target_bir_lowering=False, num_devices=1)
    aps = [nc.dram_tensor(n, arrays[n].shape, mybir.dt.float32, kind="ExternalInput").ap() for n in _INS]
    out = nc.dram_tensor("out", (B * S + 128, D), mybir.dt.float32, kind="ExternalOutput").ap()
    gated_xattn_moe_block(nc, *aps, out)
    r = run_bass_kernel_spmd(nc, [arrays], core_ids=[0])
    return arr(r.results[0]["out"][:B * S].reshape(B, S, D))
```

```python
import numpy as np
import concourse.bass as bass
from concourse import mybir
from contextlib import ExitStack


def gated_xattn_moe_block(nc, x, ctx_rows, ctx_cols, gates, gate_w, bias, shared_up, shared_down, expert_w, out):
    fp32, bf16, u32 = mybir.dt.float32, mybir.dt.bfloat16, mybir.dt.uint32
    fp32r = mybir.dt.float32r
    ALU, ACT, AX = mybir.AluOpType, mybir.ActivationFunctionType, mybir.AxisListType

    P = 128
    D = 256
    S = 64
    E, G, K = 32, 8, 4
    EG = E // G
    TOKENS = x.shape[0] * P * x.shape[2] // D
    TILES = TOKENS // P
    J = 4
    GROUPS = TILES // J
    TG = J * P
    HS = 512
    HC = HS // P
    DC = D // P
    ROW = D + E
    EPS = 1e-5
    ROUTED_SCALE = 2.5
    BIG, LOW = 3.0e38, -3.0e38
    RING = 4

    BEFORE_EXPERTS = 3
    EARLY = 2
    FILL = 2, 5, 2, 3, 2, 4

    tok_rows = nc.dram_tensor("tok_rows", (TOKENS + P, ROW), fp32, kind="Internal").ap()

    ctx = ExitStack()
    with ctx:
        def sb(name, shape, dt=fp32):
            return ctx.enter_context(nc.sbuf_tensor(name, shape, dt))

        def sem(name):
            return ctx.enter_context(nc.semaphore(name))

        def wait(eng, semaphore, value):
            if not isinstance(value, int) or value > 0:
                eng.wait_ge(semaphore, value)

        def wait_apart(eng, semaphore, value):
            eng.wait_ge(semaphore, value)
            eng.sem_inc(waits_carried, 1)

        def span(first, end, step):
            return first, end - step + 1, step

        ident = sb("ident", [P, P])
        tri = sb("tri", [P, P], bf16)
        ones = sb("ones", [P, P], bf16)
        slot_col = sb("slot_col", [P, 1])
        spare_col = sb("spare_col", [P, 1])
        slot_row = sb("slot_row", [P, P])
        block_tri = sb("block_tri", [P, P], bf16)
        minus_half = sb("minus_half", [P, J])
        zeros = sb("zeros", [P, ROW])
        biasb = sb("biasb", [P, E])
        gin = sb("gin", [P, 2])
        tg = sb("tg", [P, 2])
        wscale = sb("wscale", [P, 1])
        gwT = sb("gwT", [P, DC, E])
        su2 = [sb(f"su2_{i}", [P, DC, HS], fp32r) for i in range(2)]
        sdT = sb("sdT", [P, HC, D])
        PARTS = (0, 0), (1, 0), (0, 1)

        rows_all = sb("rows_all", [P, TILES, D])
        c4 = [sb(f"c4_{i}", [P, J, D]) for i in range(2)]
        ct4 = [sb(f"ct4_{i}", [P, J, DC, P]) for i in range(2)]
        q4 = [sb(f"q4_{i}", [P, 2, J, D]) for i in range(2)]
        sig_all = sb("sig_all", [P, 2, 2, DC, D])
        sig = [sig_all[:, i] for i in range(2)]
        rows = [sb(f"rows_{i}", [P, J, ROW]) for i in range(2)]
        xt4 = [sb(f"xt4_{i}", [P, DC, TG]) for i in range(2)]
        xt_all = sb("xt_all", [P, DC, TOKENS])
        stats1 = [sb(f"stats1_{i}", [P, J, 6]) for i in range(2)]
        mv1 = [sb(f"mv1_{i}", [P, J, 2]) for i in range(2)]
        ve1 = sb("ve1", [P, J])
        rstd1 = [sb(f"rstd1_{i}", [P, J]) for i in range(2)]
        neg1 = sb("neg1", [P, J])
        shift1 = [sb(f"shift1_{i}", [P, J]) for i in range(2)]
        stats2 = sb("stats2", [P, J, 6])
        mv2 = [sb(f"mv2_{i}", [P, J, 2]) for i in range(2)]
        ve2 = sb("ve2", [P, J])
        rstd2 = [sb(f"rstd2_{i}", [P, J]) for i in range(2)]
        scores = [sb(f"scores_{i}", [P, J, E]) for i in range(2)]
        biased = sb("biased", [P, J, E])
        pair_max = sb("pair_max", [P, J * G, 2])
        pair_sum = sb("pair_sum", [P, J * G, 2])
        cross_sum = sb("cross_sum", [P, J * G])
        same_sum = sb("same_sum", [P, J * G])
        group_in = sb("group_in", [P, J, G + K])
        group_top = sb("group_top", [P, J, 8])
        group_rep = sb("group_rep", [P, J, 8])
        group_out = sb("group_out", [P, J, G + K])
        group_sel = sb("group_sel", [P, J * G])
        masked = sb("masked", [P, J * G, EG])
        exp_in = sb("exp_in", [P, J, E + K])
        exp_top = sb("exp_top", [P, J, 8])
        exp_rep = sb("exp_rep", [P, J, 8])
        exp_out = sb("exp_out", [P, J, E + K])
        picked = sb("picked", [P, J, E])
        pick_sum = sb("pick_sum", [P, J])
        pick_inv = sb("pick_inv", [P, J])
        sel_all = sb("sel_all", [P, TILES, E], bf16)

        relu_h = [sb(f"relu_h_{i}", [P, TG]) for i in range(2)]
        xs2 = [sb(f"xs2_{i}", [P, 2, DC, TG], fp32r) for i in range(2)]
        hT = sb("hT", [P, HC, TG])
        tile_picks = sb("tile_picks", [P, 8], bf16)
        marks = sb("marks", [P, 8, 4], bf16)
        slot_marks = sb("slot_marks", [P, E, 4])
        rank_half = sb("rank_half", [P, E])
        in_sign = sb("in_sign", [P, E])
        rank = sb("rank", [P, E])
        bounds = sb("bounds", [P, 2, 8])
        su_raw = xt_all[:, :, (GROUPS - 1) * TG:GROUPS * TG]
        from_lo = q4[0][:, 0, :, :].rearrange("p j (k q) -> p (j k) q", q=P)
        onehot = sb("onehot", [P, 8, P], bf16)
        prefix = sb("prefix", [P, 8, P], bf16)
        compared = sig_all[:, :, :, :, :].rearrange("p i b c d -> p (i b c d)").bitcast(bf16).rearrange("p (e t) -> p e t", t=P)
        in_tile = sb("in_tile", [P, E])
        tok_a = sb("tok_a", [P, E])
        tok_b = sb("tok_b", [P, E])
        tok_c = sb("tok_c", [P, E])
        tok_id = sb("tok_id", [P, E], u32)
        slot_tok = sb("slot_tok", [P, 8], u32)
        wring = [ct4[i // 2][:, 2 * (i % 2):2 * (i % 2) + 2, :, :].rearrange("p j c q -> p (j c q)") for i in range(RING)]
        xe = [sb(f"xe_{i}", [P, ROW]) for i in range(RING)]
        xeT = [sb(f"xeT_{i}", [P, DC, P]) for i in range(2)]
        relu_e = sb("relu_e", [P, P])
        h_e = [sb(f"h_e_{i}", [P, P]) for i in range(2)]
        y_e = [sb(f"y_e_{i}", [P, D]) for i in range(2)]

        psum = ctx.enter_context(nc.psum_tensor("psum", [P, 8 * 512], fp32))
        bank = [psum[:, 512 * i:512 * i + 512] for i in range(8)]
        logits = [psum[:, 1024 * i:1024 * i + 1024] for i in range(2)]

        waits_carried = sem("waits_carried")
        params_loaded = sem("params_loaded")
        shared_loaded = sem("shared_loaded")
        dump_rows_zeroed = sem("dump_rows_zeroed")
        pool_self = sem("pool_self")
        norm1_self = sem("norm1_self")
        norm2_self = sem("norm2_self")
        index_copied = sem("index_copied")
        q_zeroed = sem("q_zeroed")
        consts_ready = sem("consts_ready")
        zeros_ready = sem("zeros_ready")
        tanh_ready = sem("tanh_ready")
        x_loaded = [sem(f"x_loaded_{i}") for i in range(2)]
        ctx_loaded = [sem(f"ctx_loaded_{i}") for i in range(2)]
        stats1_ready = sem("stats1_ready")
        rstd1_ready = sem("rstd1_ready")
        q_ready = sem("q_ready")
        logits_ready = sem("logits_ready")
        sig_ready = sem("sig_ready")
        pv_ready = sem("pv_ready")
        x1_ready = sem("x1_ready")
        stats2_ready = sem("stats2_ready")
        rstd2_ready = sem("rstd2_ready")
        xn_ready = sem("xn_ready")
        xt_in_psum = sem("xt_in_psum")
        xt_ready = sem("xt_ready")
        gate_ready = sem("gate_ready")
        scores_ready = sem("scores_ready")
        routed = sem("routed")
        x1_stored = [sem(f"x1_stored_{i}") for i in range(2)]
        rows_stored = [sem(f"rows_stored_{i}") for i in range(2)]
        dve_self = sem("dve_self")
        tile_picks_ready = sem("tile_picks_ready")
        prefix_ready = sem("prefix_ready")
        bounds_in_psum = sem("bounds_in_psum")
        onehot_ready = sem("onehot_ready")
        prefix_copied = sem("prefix_copied")
        counts_ready = sem("counts_ready")
        tables_set = sem("tables_set")
        bounds_copied = sem("bounds_copied")
        slot_bases_ready = sem("slot_bases_ready")
        slot_marks_in_psum = sem("slot_marks_in_psum")
        slot_marks_read = sem("slot_marks_read")
        ranks_ready = sem("ranks_ready")
        counted_dve = sem("counted_dve")
        counted_act = sem("counted_act")
        table_ready = sem("table_ready")
        up_ready = sem("up_ready")
        relu_done = sem("relu_done")
        weights_hi_ready = sem("weights_hi_ready")
        weights_lo_ready = sem("weights_lo_ready")
        xs_hi_ready = sem("xs_hi_ready")
        xs_lo_ready = sem("xs_lo_ready")
        h_ready = sem("h_ready")
        y_ready = sem("y_ready")
        y_kept = sem("y_kept")
        weights_loaded = [sem(f"weights_loaded_{i}") for i in range(RING)]
        gathered = [sem(f"gathered_{i}") for i in range(RING)]
        xe_in_psum = sem("xe_in_psum")
        xeT_ready = sem("xeT_ready")
        he_in_psum = sem("he_in_psum")
        he_read = sem("he_read")
        he_ready = sem("he_ready")
        ye_in_psum = sem("ye_in_psum")
        ye_ready = sem("ye_ready")
        scattered = sem("scattered")
        shared_added = sem("shared_added")

        block = ctx.enter_context(nc.Block())

        tok_groups = tok_rows[0:TOKENS].rearrange("(g j p) d -> g p j d", j=J, p=P)
        out_groups = out[0:TOKENS].rearrange("(g j p) d -> g p j d", j=J, p=P)


        def nth(b, par):
            return b - par

        def xt_bank(b, dc):
            return bank[4 if dc == 1 and isinstance(b, int) and b == GROUPS - 1 else 6][:, :]

        def rows_t(n):
            return xt_all[:, :, bass.ds(n * TG, TG)]

        def split_t(part, n):
            return xs2[part][:, bass.ds(n % 2, 1), :, :].rearrange("p b c t -> p (b c) t")

        def split_rows_low(eng, n):
            eng.wait_ge(xs_hi_ready, n + 1)
            eng.tensor_tensor(split_t(1, n), rows_t(n), split_t(0, n), ALU.subtract).then_inc(xs_lo_ready, 1)

        def has(n, count=GROUPS):
            return not isinstance(n, int) or n < count

        @block.sync
        def _(sp):
            def tiles(b):
                return rows_all[:, bass.ds(b * J, J), :]

            def load_x(b, par):
                sp.dma_start(tiles(b).rearrange("p j d -> p (j d)"), x[bass.ds(b, 1)].rearrange("g p f -> p (g f)")).then_inc(x_loaded[par], 16)

            def load_ctx_rows(b, par):
                sp.dma_start(c4[par][:, :, :].rearrange("p j d -> p (j d)"), ctx_rows[bass.ds(b, 1)].rearrange("g p f -> p (g f)")).then_inc(ctx_loaded[par], 16)

            def load_ctx_cols(b, par):
                sp.dma_start(ct4[par][:, :, :, :].rearrange("p j c d -> p (j c d)"), ctx_cols[bass.ds(b, 1)].rearrange("g p f -> p (g f)")).then_inc(ctx_loaded[par], 16)

            load_x(0, 0)
            sp.dma_start(gin[:, :], gates).then_inc(params_loaded, 16)
            load_ctx_rows(0, 0)
            load_ctx_cols(0, 0)
            sp.dma_start(biasb[:, :], bias).then_inc(params_loaded, 16)
            sp.dma_start(gwT[:, :, :].rearrange("p c e -> p (c e)"), gate_w).then_inc(params_loaded, 16)
            load_x(1, 1)
            load_ctx_rows(1, 1)
            load_ctx_cols(1, 1)
            sp.wait_ge(zeros_ready, 1)
            sp.dma_start(tok_rows[TOKENS:TOKENS + P], zeros[:, :]).then_inc(dump_rows_zeroed, 16)
            sp.dma_start(out[TOKENS:TOKENS + P], zeros[:, 0:D]).then_inc(dump_rows_zeroed, 16)
            sp.dma_start(su_raw, shared_up.rearrange("p (c h) -> p c h", h=TG)).then_inc(shared_loaded, 16)
            sp.dma_start(sdT[:, :, :].rearrange("p c e -> p (c e)"), shared_down).then_inc(shared_loaded, 16)

            def store_x1(b, par):
                sp.wait_ge(x1_ready, J * b + J)
                sp.dma_start(out_groups[bass.ds(b, 1)].rearrange("g p j d -> p (g j) d"), tiles(b)).then_inc(x1_stored[par], 16)

            def store_rows(b, par):
                sp.wait_ge(routed, b + 1)
                sp.dma_start(tok_groups[bass.ds(b, 1)].rearrange("g p j d -> p (g j) d"), rows[par][:, :, :]).then_inc(rows_stored[par], 16)

            def step(s, h, live):
                now, prev, prev2 = live
                if now and (not isinstance(s, int) or s + 2 < GROUPS):
                    sp.wait_ge(stats1_ready, s + 1)
                    load_x(s + 2, h)
                if prev:
                    if not isinstance(s, int) or s + 1 < GROUPS:
                        sp.wait_ge(logits_ready, J * s)
                        load_ctx_rows(s + 1, 1 - h)
                        sp.wait_ge(pv_ready, J * s)
                        load_ctx_cols(s + 1, 1 - h)
                    store_x1(s - 1, 1 - h)
                if prev2:
                    store_rows(s - 2, h)

            step(0, 0, (True, False, False))
            step(1, 1, (True, True, False))
            with sp.Fori(*span(2, GROUPS - 2, 2)) as s:
                for h in range(2):
                    step(s + h, h, (True, True, True))
            step(GROUPS - 2, 0, (True, True, True))
            step(GROUPS - 1, 1, (True, True, True))
            step(GROUPS, 0, (False, True, True))
            step(GROUPS + 1, 1, (False, False, True))

            def load_weights(e, r):
                sp.dma_start(wring[r], expert_w[bass.ds(e, 1)].rearrange("e p f -> p (e f)")).then_inc(weights_loaded[r], 16)

            sp.wait_ge(pv_ready, TILES)
            for r in range(RING):
                load_weights(r, r)
            with sp.Fori(*span(0, E - RING, RING)) as e0:
                for r in range(RING):
                    sp.wait_ge(ye_in_psum, e0 + r + 1)
                    load_weights(e0 + r + RING, r)

        @block.gpsimd
        def _(pool):
            pool.memset(zeros[:, :], 0.0).then_inc(zeros_ready, 1)
            pool.memset(ident[:, :], 0.0).then_inc(pool_self, 1)
            pool.memset(minus_half[:, :], -0.5).then_inc(pool_self, 1)
            pool.wait_ge(pool_self, 2)
            pool.affine_select(out=ident[:, :], in_=ident[:, :], compare_op=ALU.not_equal, fill=1.0, base=0,
                               pattern=[[-1, P]], channel_multiplier=1).then_inc(consts_ready, 1)
            pool.memset(ones[:, :], 1.0).then_inc(consts_ready, 1)
            pool.wait_ge(consts_ready, 2)
            pool.affine_select(out=tri[:, :], in_=ones[:, :], compare_op=ALU.is_ge, fill=0.0, base=0,
                               pattern=[[1, P]], channel_multiplier=-1).then_inc(consts_ready, 1)
            pool.iota(slot_col[:, :], pattern=[[0, 1]], base=0, channel_multiplier=1,
                      allow_small_or_imprecise_dtypes=True).then_inc(consts_ready, 1)
            pool.iota(slot_row[:, :], pattern=[[1, P]], base=0, channel_multiplier=0,
                      allow_small_or_imprecise_dtypes=True).then_inc(consts_ready, 1)

            def norm1(b, par):
                wait_apart(pool, stats1_ready, b + 1)
                pool.tensor_scalar(ve1[:, :], mv1[par][:, :, 1], EPS, None, op0=ALU.add).then_inc(norm1_self, 1)
                pool.tensor_scalar(neg1[:, :], mv1[par][:, :, 0], -1.0, None, op0=ALU.mult).then_inc(norm1_self, 1)
                pool.wait_ge(norm1_self, 3 * b + 2)
                pool.tensor_tensor(rstd1[par][:, :], ve1[:, :], minus_half[:, :], ALU.pow).then_inc(norm1_self, 1)
                pool.wait_ge(norm1_self, 3 * b + 3)
                pool.tensor_tensor(shift1[par][:, :], neg1[:, :], rstd1[par][:, :], ALU.mult).then_inc(rstd1_ready, 1)

            def norm2(b, par):
                wait_apart(pool, stats2_ready, b + 1)
                pool.tensor_scalar(ve2[:, :], mv2[par][:, :, 1], EPS, None, op0=ALU.add).then_inc(norm2_self, 1)
                pool.wait_ge(norm2_self, b + 1)
                pool.tensor_tensor(rstd2[par][:, :], ve2[:, :], minus_half[:, :], ALU.pow).then_inc(rstd2_ready, 1)

            norm1(0, 0)
            pool.affine_select(out=block_tri[:, :].rearrange("p (q i) -> p q i", i=TILES),
                               in_=tri[:, :].rearrange("p (q i) -> p q i", i=TILES), compare_op=ALU.is_ge, fill=0.0, base=0,
                               pattern=[[-TILES, 4], [0, TILES]], channel_multiplier=1).then_inc(tables_set, 1)
            pool.iota(spare_col[:, :], pattern=[[0, 1]], base=TOKENS, channel_multiplier=1,
                      allow_small_or_imprecise_dtypes=True).then_inc(tables_set, 1)
            pool.memset(marks[:, :, :], 1.0).then_inc(tables_set, 1)
            for q in range(4):
                pool.wait_ge(tables_set, 3 + q)
                pool.iota(marks[32 * q:32 * q + 32, :, 1], pattern=[[0, 8]], base=0, channel_multiplier=1,
                          allow_small_or_imprecise_dtypes=True).then_inc(tables_set, 1)
            pool.wait_ge(tables_set, 7)
            norm1(1, 1)
            norm2(0, 0)
            norm1(2, 0)
            pool.wait_ge(weights_hi_ready, 1)
            pool.tensor_tensor(su2[1][:, :, :], su_raw, su2[0][:, :, :], ALU.subtract).then_inc(weights_lo_ready, 1)
            norm2(1, 1)
            with pool.Fori(*span(2, GROUPS - 2, 2)) as b:
                for h in range(2):
                    norm1(b + h + 1, 1 - h)
                    norm2(b + h, h)
            norm1(GROUPS - 1, 1)
            norm2(GROUPS - 2, 0)
            split_rows_low(pool, 0)
            norm2(GROUPS - 1, 1)
            for n in range(1, BEFORE_EXPERTS + 1):
                split_rows_low(pool, n)


            def gather(e, r):
                pool.tensor_copy(slot_tok[:, r % 8:r % 8 + 1], tok_id[:, bass.ds(e, 1)]).then_inc(index_copied, 1)
                wait_apart(pool, index_copied, e + 1)
                pool.indirect_dma_start(xe[r % RING][:, :], None, tok_rows,
                                        bass.IndirectOffsetOnAxis(ap=slot_tok[:, r % 8:r % 8 + 1], axis=0)).then_inc(gathered[r % RING], 16)

            def scatter(e, r):
                wait_apart(pool, ye_ready, e + 1)
                pool.indirect_dma_start(out, bass.IndirectOffsetOnAxis(ap=slot_tok[:, r % 8:r % 8 + 1], axis=0),
                                        y_e[r % 2][:, :], None, compute_op=ALU.add).then_inc(scattered, 16)

            pool.wait_ge(table_ready, 1)
            pool.wait_ge(dump_rows_zeroed, 32)
            for par in range(2):
                pool.wait_ge(rows_stored[par], 16 * GROUPS // 2)
                pool.wait_ge(x1_stored[par], 16 * GROUPS // 2)
            for r in range(RING):
                gather(r, r)

            def add_shared(n):
                wait(pool, y_kept, J * n + J)
                pool.dma_start(out_groups[n], rows_all[:, n * J:n * J + J, :], accum_op=ALU.add).then_inc(shared_added, 16)

            for n in range(EARLY):
                add_shared(n)
            pool.wait_ge(shared_added, 16 * EARLY)

            def slots(e0, last_):
                for r in range(8):
                    scatter(e0 + r, r)
                    if not (last_ and r >= 8 - RING):
                        gather(e0 + r + RING, r + RING)
                    wait_apart(pool, scattered, 16 * e0 + 16 * (r + 1))

            with pool.Fori(*span(0, E - 8, 8)) as e0:
                slots(e0, False)
            slots(E - 8, True)
            for n in range(EARLY, GROUPS):
                add_shared(n)
            pool.wait_ge(shared_added, 16 * GROUPS)

        @block.scalar
        def _(act):
            act.wait_ge(params_loaded, 48)
            nc.scalar.activation(tg[:, :], gin[:, :], ACT.Tanh).then_inc(tanh_ready, 1)

            def normed_queries(b, par, j):
                if j == 0:
                    act.wait_ge(rstd1_ready, b + 1)
                for k in range(2):
                    own_rows = slice(S * k, S * k + S)
                    last = nc.scalar.activation(q4[par][own_rows, k, j, :], rows_all[own_rows, bass.ds(b * J + j, 1), :].rearrange("p t d -> p (t d)"),
                                                ACT.Identity, bias=shift1[par][own_rows, j:j + 1], scale=rstd1[par][own_rows, j:j + 1])
                last.then_inc(q_ready, 1)

            def sigmoid(s, j):
                t = s * J + j
                act.wait_ge(logits_ready, t + 1)
                wait(act, pv_ready, t - 1)
                nc.scalar.activation(sig[j % 2][:, :, :, :].rearrange("p b c m -> p (b c m)"), logits[j % 2], ACT.Sigmoid,
                                     scale=float(S) ** -0.5).then_inc(sig_ready, 1)

            def copy_xt(b, par, dc):
                act.wait_ge(xt_in_psum, 2 * b + dc + 1)
                nc.scalar.copy(xt4[par][:, dc, :], xt_bank(b, dc))
                nc.scalar.copy(xt_all[:, dc, bass.ds(b * TG, TG)], xt_bank(b, dc)).then_inc(xt_ready, 1)

            def score(b, par):
                act.wait_ge(gate_ready, b + 1)
                nc.scalar.activation(scores[par][:, :, :].rearrange("p j e -> p (j e)"), bank[7][:, 0:J * E],
                                     ACT.Sigmoid).then_inc(scores_ready, 1)

            def step(s, h, live):
                now, prev, prev2 = live
                more = now and (not isinstance(s, int) or s + 1 < GROUPS)
                if now:
                    sigmoid(s, 0)
                if prev2:
                    score(s - 2, h)
                if now:
                    sigmoid(s, 1)
                if more:
                    normed_queries(s + 1, 1 - h, 0)
                    normed_queries(s + 1, 1 - h, 1)
                if now:
                    sigmoid(s, 2)
                if prev:
                    copy_xt(s - 1, 1 - h, 0)
                if more:
                    normed_queries(s + 1, 1 - h, 2)
                    normed_queries(s + 1, 1 - h, 3)
                if now:
                    sigmoid(s, 3)
                if prev:
                    copy_xt(s - 1, 1 - h, 1)

            def relu(n, c):
                u = HC * n + c
                act.wait_ge(up_ready, u + 1)
                wait(act, h_ready, u - 1)
                nc.scalar.activation(relu_h[c % 2][:, :], bank[c % 2][:, :], ACT.Relu).then_inc(relu_done, 1)

            def square(n, c):
                act.wait_ge(relu_done, HC * n + c + 1)
                nc.scalar.activation(hT[:, c, :], relu_h[c % 2][:, :], ACT.Square).then_inc(h_ready, 1)

            def split_weights_high():
                act.wait_ge(shared_loaded, 32)
                nc.scalar.copy(su2[0][:, :, :], su_raw).then_inc(weights_hi_ready, 1)

            def split_rows_high(n):
                act.wait_ge(xt_ready, 2 * n + 2)
                nc.scalar.copy(split_t(0, n), rows_t(n)).then_inc(xs_hi_ready, 1)

            def down_tile(n, j):
                t = J * n + j
                act.wait_ge(y_ready, t + 1)
                nc.scalar.activation(rows_all[:, bass.ds(t, 1), :].rearrange("p t d -> p (t d)"), bank[2 + j % 2][:, 0:D],
                                     ACT.Copy, scale=tg[:, 1:2]).then_inc(y_kept, 1)

            def piece(n, k):
                if k < HC - 2:
                    relu(n, k + 2)
                    square(n, k + 2)
                elif k < HC:
                    if has(n + 1):
                        relu(n + 1, k - (HC - 2))
                else:
                    if k == HC and has(n + 2):
                        split_rows_high(n + 2)
                    down_tile(n, k - HC)
                    if k == 2 * HC - 1 and has(n + 1):
                        square(n + 1, 0)
                        square(n + 1, 1)

            for j in range(J):
                normed_queries(0, 0, j)
            step(0, 0, (True, False, False))
            split_weights_high()
            step(1, 1, (True, True, False))
            with act.Fori(*span(2, GROUPS - 2, 2)) as s:
                for h in range(2):
                    step(s + h, h, (True, True, True))
            step(GROUPS - 2, 0, (True, True, True))
            split_rows_high(0)
            step(GROUPS - 1, 1, (True, True, True))
            pieces = [(n, k) for n in range(BEFORE_EXPERTS) for k in range(8)]

            def follow(count):
                for _ in range(count):
                    n, k = pieces.pop(0)
                    if (n, k) == (0, HC):
                        for par in range(2):
                            act.wait_ge(x1_stored[par], 16 * GROUPS // 2)
                    piece(n, k)

            score(GROUPS - 2, 0)
            split_rows_high(1)
            for c in range(2):
                relu(0, c)
                square(0, c)
            follow(1)
            copy_xt(GROUPS - 1, 1, 0)
            copy_xt(GROUPS - 1, 1, 1)
            follow(FILL[0])
            score(GROUPS - 1, 1)

            follow(FILL[1])
            act.wait_ge(tile_picks_ready, 1)
            for half in range(2):
                last = nc.scalar.copy(prefix[:, 4 * half:4 * half + 4, :].rearrange("p k q -> p (k q)"), bank[6 + half][:, :])
            last.then_inc(prefix_copied, 1)
            follow(FILL[2] + FILL[3])
            for r in range(2):
                if r == 0:
                    act.wait_ge(ranks_ready, 1)
                for i, q in ((1, 2), (3, 3)):
                    act.wait_ge(counts_ready, 4 * r + i + 1)
                    for k in range(4):
                        e = 16 * r + 4 * k + q
                        last = nc.scalar.activation(compared[:, e, :], bank[4 + q][:, k * P:k * P + P], ACT.Sign,
                                                    scale=-1.0, bias=rank_half[:, e:e + 1], accum_out=in_sign[:, e:e + 1])
                    last.then_inc(counted_act, 1)
                follow(FILL[4] if r == 0 else len(pieces))
            with act.Fori(BEFORE_EXPERTS, GROUPS - 2) as n:
                for k in range(8):
                    piece(n, k)
            for n in range(GROUPS - 2, GROUPS):
                for k in range(8):
                    piece(n, k)

        @block.tensor
        def _(pe):
            pe.wait_ge(consts_ready, 5)

            def qk(s, h, j):
                t = s * J + j
                if j == 0:
                    pe.wait_ge(ctx_loaded[h], 16 * nth(s, h) + 32)
                pe.wait_ge(q_ready, t + 1)
                wait(pe, sig_ready, t - 1)
                for half in range(DC):
                    for b in range(2):
                        last = nc.tensor.matmul(bank[2 * (j % 2) + b][:, half * D:half * D + D],
                                                q4[h][:, b, j, half * P:half * P + P], c4[h][:, j, :],
                                                start=True, stop=True)
                last.then_inc(logits_ready, 1)

            def pv(s, h, j):
                t = s * J + j
                pe.wait_ge(sig_ready, t + 1)
                wait(pe, x1_ready, t - 1)
                for half in range(DC):
                    for b in range(2):
                        last = nc.tensor.matmul(bank[4 + j % 2][S * b:S * b + S, 0:D],
                                                ct4[h][:, j, half, S * b:S * b + S], sig[j % 2][:, b, half, :],
                                                start=(half == 0), stop=(half == DC - 1))
                last.then_inc(pv_ready, 1)

            def transpose_rows(b, par, dc):
                pe.wait_ge(xn_ready, b + 1)
                last_group = isinstance(b, int) and b == GROUPS - 1
                wait(pe, xt_ready, 2 * b + (0 if last_group else dc))
                for j in range(J):
                    last = nc.tensor.transpose(xt_bank(b, dc)[:, j * P:j * P + P], rows[par][:, j, dc * P:dc * P + P], ident[:, :])
                last.then_inc(xt_in_psum, 1)

            def gate(b, par):
                pe.wait_ge(xt_ready, 2 * b + 2)
                for j in range(J):
                    for dc in range(DC):
                        last = nc.tensor.matmul(bank[7][:, j * E:j * E + E], xt4[par][:, dc, j * P:j * P + P],
                                                gwT[:, dc, :], start=(dc == 0), stop=(dc == DC - 1))
                last.then_inc(gate_ready, 1)

            def step(s, h, live):
                now, prev, prev2 = live
                if now:
                    qk(s, h, 0)
                if prev:
                    pv(s - 1, 1 - h, J - 1)
                if prev2:
                    gate(s - 2, h)
                if now:
                    qk(s, h, 1)
                    pv(s, h, 0)
                    qk(s, h, 2)
                    pv(s, h, 1)
                if prev:
                    transpose_rows(s - 1, 1 - h, 0)
                if now:
                    qk(s, h, 3)
                    pv(s, h, 2)
                if prev:
                    transpose_rows(s - 1, 1 - h, 1)

            def prefixes():
                pe.wait_ge(routed, GROUPS)
                pe.wait_ge(xt_ready, 2 * GROUPS)
                for k in range(8):
                    for q in range(4):
                        last = nc.tensor.matmul(bank[6 + k // 4][32 * q:32 * q + 32, (k % 4) * P:(k % 4) * P + P],
                                                sel_all[:, :, 4 * k + q], tri[:, :], start=True, stop=True,
                                                tile_position=(0, 32 * q))
                last.then_inc(prefix_ready, 1)

            def bounds_up():
                pe.wait_ge(tile_picks_ready, 1)
                nc.tensor.matmul(bank[4][:, 0:8], block_tri[:, :], tile_picks[:, :], start=True, stop=True).then_inc(bounds_in_psum, 1)

            def slot_tiles():
                pe.wait_ge(onehot_ready, 1)
                pe.wait_ge(slot_bases_ready, 1)
                pe.wait_ge(prefix_copied, 1)
                for e in range(E):
                    q, k = e % 4, e // 4
                    last = nc.tensor.matmul(bank[4 + q][:, 4 * k:4 * k + 4], onehot[32 * q:32 * q + 32, k, :],
                                            marks[32 * q:32 * q + 32, k, :], start=True, stop=True, tile_position=(32 * q, 0))
                last.then_inc(slot_marks_in_psum, 1)

            def counts(r):
                if r == 0:
                    pe.wait_ge(slot_marks_read, 1)
                for i, q in enumerate((0, 2, 1, 3)):
                    if r == 1:
                        pe.wait_ge(counted_act if q >= 2 else counted_dve, 1 + q % 2)
                    for k in range(4):
                        kk = 4 * r + k
                        last = nc.tensor.matmul(bank[4 + q][:, k * P:k * P + P], onehot[32 * q:32 * q + 32, kk, :],
                                                prefix[32 * q:32 * q + 32, kk, :], start=True, stop=True,
                                                tile_position=(32 * q, 0))
                    last.then_inc(counts_ready, 1)

            def up_chunk(n, c):
                u = HC * n + c
                wait(pe, relu_done, u - 1)
                if c == 0:
                    pe.wait_ge(xs_lo_ready, n + 1)
                for i, (dc, (a, b)) in enumerate((dc, parts) for parts in PARTS for dc in range(DC)):
                    rows_part = xs2[b][:, bass.ds(n % 2, 1), dc, :].rearrange("p b t -> p (b t)")
                    last = nc.tensor.matmul(bank[c % 2][:, :], su2[a][:, dc, c * P:c * P + P], rows_part,
                                            start=(i == 0), stop=(i == 3 * DC - 1))
                last.then_inc(up_ready, 1)

            def down_tile(n, j):
                t = J * n + j
                pe.wait_ge(h_ready, HC * n + HC)
                wait(pe, y_kept, t - 1)
                for c in range(HC):
                    last = nc.tensor.matmul(bank[2 + j % 2][:, 0:D], hT[:, c, j * P:j * P + P], sdT[:, c, :],
                                            start=(c == 0), stop=(c == HC - 1))
                last.then_inc(y_ready, 1)

            def shared_piece(n, k):
                if k < HC - 2:
                    up_chunk(n, k + 2)
                elif k < HC:
                    if has(n + 1):
                        up_chunk(n + 1, k - (HC - 2))
                else:
                    down_tile(n, k - HC)

            def rows_T(e, r):
                pe.wait_ge(gathered[r % RING], 16 * ((e - r % RING) // RING) + 16 if isinstance(e, int) else 4 * (e - r % RING) + 16)
                wait(pe, xeT_ready, e)
                for dc in range(DC):
                    last = nc.tensor.transpose(bank[4][:, dc * P:dc * P + P], xe[r % RING][:, dc * P:dc * P + P], ident[:, :])
                last.then_inc(xe_in_psum, 1)

            def expert_up(e, r):
                pe.wait_ge(weights_loaded[r % RING], 16 * ((e - r % RING) // RING) + 16 if isinstance(e, int) else 4 * (e - r % RING) + 16)
                pe.wait_ge(xeT_ready, e + 1)
                wait(pe, he_ready, e)
                for dc in range(DC):
                    last = nc.tensor.matmul(bank[5][:, 0:P], wring[r % RING][:, dc * P:dc * P + P], xeT[r % 2][:, dc, :],
                                            start=(dc == 0), stop=(dc == DC - 1))
                last.then_inc(he_in_psum, 1)

            def expert_down(e, r):
                pe.wait_ge(he_ready, e + 1)
                wait(pe, ye_ready, e)
                nc.tensor.matmul(bank[6][:, 0:D], h_e[r % 2][:, :], wring[r % RING][:, D:2 * D],
                                 start=True, stop=True).then_inc(ye_in_psum, 1)

            pe.wait_ge(params_loaded, 48)
            pe.wait_ge(q_zeroed, 2)
            step(0, 0, (True, False, False))
            pe.wait_ge(q_zeroed, 4)
            step(1, 1, (True, True, False))
            with pe.Fori(*span(2, GROUPS, 2)) as s:
                for h in range(2):
                    step(s + h, h, (True, True, True))

            pieces = [(n, k) for n in range(BEFORE_EXPERTS) for k in range(8)]

            def fill(count):
                for _ in range(count):
                    shared_piece(*pieces.pop(0))

            pe.wait_ge(weights_lo_ready, 1)
            pv(GROUPS - 1, 1, J - 1)
            gate(GROUPS - 2, 0)
            pe.wait_ge(sig_ready, TILES)
            up_chunk(0, 0)
            up_chunk(0, 1)
            fill(1)
            transpose_rows(GROUPS - 1, 1, 0)
            transpose_rows(GROUPS - 1, 1, 1)
            fill(FILL[0])
            gate(GROUPS - 1, 1)
            fill(FILL[1])
            pe.wait_ge(tables_set, 7)
            prefixes()
            fill(FILL[2])
            bounds_up()
            fill(FILL[3])
            slot_tiles()
            counts(0)
            fill(FILL[4])
            counts(1)
            fill(FILL[5])

            rows_T(0, 0)

            def slots(n, e0, first, last_):
                for k in range(8):
                    e = e0 + k
                    expert_up(e, k)
                    if not (last_ and k == 7):
                        rows_T(e + 1, k + 1)
                    if not (first and k == 0):
                        expert_down(e - 1, k + 7)
                    if first:
                        fill(2 if len(pieces) > 8 - k else 1)
                    else:
                        shared_piece(n, k)

            pieces += [(BEFORE_EXPERTS, k) for k in range(8)]
            slots(BEFORE_EXPERTS, 0, True, False)
            with pe.Fori(BEFORE_EXPERTS + 1, BEFORE_EXPERTS + 3) as n:
                slots(n, n * 8 - BEFORE_EXPERTS * 8, False, False)
            slots(BEFORE_EXPERTS + 3, E - 8, False, True)
            expert_down(E - 1, 7)
            for n in range(BEFORE_EXPERTS + 4, GROUPS):
                for k in range(8):
                    shared_piece(n, k)

        @block.vector
        def _(dve):
            V = nc.vector

            class Own:
                def __init__(self):
                    self.base, self.n = 0, 0

                def mark(self, instruction):
                    instruction.then_inc(dve_self, 1)
                    self.n += 1

                def wait(self):
                    dve.wait_ge(dve_self, self.base + self.n)

                def wait_apart(self):
                    wait_apart(dve, dve_self, self.base + self.n)

            own = Own()

            def zero_beside(par):
                for k in range(2):
                    other = slice(S * (1 - k), S * (1 - k) + S)
                    V.memset(q4[par][other, k, :, :], 0.0).then_inc(q_zeroed, 1)

            zero_beside(0)
            own.mark(V.memset(group_in[:, :, :], LOW))
            own.mark(V.memset(group_rep[:, :, :], LOW))
            own.mark(V.memset(exp_in[:, :, :], LOW))
            own.mark(V.memset(exp_rep[:, :, :], LOW))

            def tile(t, part=slice(0, P)):
                return rows_all[part, bass.ds(t, 1), :].rearrange("p t d -> p (t d)")

            def norm1_stats(b, par):
                wait_apart(dve, x_loaded[par], 8 * nth(b, par) + 16)
                for j in range(J):
                    own.mark(V.bn_stats(stats1[par][:, j, :], tile(b * J + j)))
                own.wait_apart()
                for j in range(J):
                    last = V.bn_aggr(mv1[par][:, j, :], stats1[par][:, j, :])
                last.then_inc(stats1_ready, 1)

            def residual(s, h, j):
                t = s * J + j
                dve.wait_ge(pv_ready, t + 1)
                V.scalar_tensor_tensor(tile(t), bank[4 + j % 2][:, 0:D], tg[:, 0:1], tile(t),
                                       op0=ALU.mult, op1=ALU.add).then_inc(x1_ready, 1)
                wait_apart(dve, x1_ready, t + 1)
                own.mark(V.bn_stats(stats2[:, j, :], tile(t)))
                if j == J - 1:
                    own.wait_apart()
                    for k in range(J):
                        last = V.bn_aggr(mv2[h][:, k, :], stats2[:, k, :])
                    last.then_inc(stats2_ready, 1)

            def norm2_apply(b, par):
                dve.wait_ge(rstd2_ready, b + 1)
                if not isinstance(b, int) or b >= 2:
                    dve.wait_ge(rows_stored[par], 8 * nth(b, par))
                    dve.wait_ge(xt_in_psum, 2 * b - 2)
                for j in range(J):
                    last = V.tensor_scalar(rows[par][:, j, 0:D], tile(b * J + j), mv2[par][:, j, 0:1], rstd2[par][:, j:j + 1],
                                           op0=ALU.subtract, op1=ALU.mult)
                last.then_inc(xn_ready, 1)

            def do(instruction):
                own.mark(instruction)
                own.wait()

            def route_groups(b, par):
                dve.wait_ge(scores_ready, b + 1)
                sc = scores[par]
                do(V.tensor_tensor(biased[:, :, :], sc[:, :, :], biasb[:, :].unsqueeze(1).to_broadcast([P, J, E]), ALU.add))
                bv = biased[:, :, :].rearrange("p j (g a b) -> p (j g) a b", g=G, a=2)
                own.mark(V.tensor_tensor(pair_max[:, :, :], bv[:, :, :, 0], bv[:, :, :, 1], ALU.max))
                do(V.tensor_tensor(pair_sum[:, :, :], bv[:, :, :, 0], bv[:, :, :, 1], ALU.add))
                own.mark(V.tensor_tensor(cross_sum[:, :], pair_max[:, :, 0], pair_max[:, :, 1], ALU.add))
                do(V.tensor_tensor(same_sum[:, :], pair_sum[:, :, 0], pair_sum[:, :, 1], ALU.max))
                own.mark(V.tensor_tensor(group_in[:, :, 0:G], cross_sum[:, :].rearrange("p (j g) -> p j g", g=G),
                                         same_sum[:, :].rearrange("p (j g) -> p j g", g=G), ALU.max))

            def route_masks(b, par):
                own.wait_apart()
                for j in range(J):
                    own.mark(V.max(group_top[:, j, :], group_in[:, j, 0:G]))
                own.wait()
                own.mark(V.tensor_copy(group_rep[:, :, 0:K], group_top[:, :, 0:K]))
                own.wait_apart()
                for j in range(J):
                    own.mark(V.match_replace(group_out[:, j, :], group_rep[:, j, :], group_in[:, j, :], BIG))
                own.wait()
                do(V.tensor_scalar(group_sel[:, :].rearrange("p (j g) -> p j g", g=G), group_out[:, :, 0:G], BIG / 2, None, op0=ALU.is_ge))
                do(V.tensor_tensor(masked[:, :, :], biased[:, :, :].rearrange("p j (g a) -> p (j g) a", g=G),
                                   group_sel[:, :].unsqueeze(2).to_broadcast([P, J * G, EG]), ALU.mult))
                own.mark(V.tensor_scalar(exp_in[:, :, 0:E], masked[:, :, :].rearrange("p (j g) a -> p j (g a)", j=J), 0.0, None, op0=ALU.add))

            def route_experts(b, par):
                sc = scores[par]
                own.wait_apart()
                for j in range(J):
                    own.mark(V.max(exp_top[:, j, :], exp_in[:, j, 0:E]))
                own.wait()
                own.mark(V.tensor_copy(exp_rep[:, :, 0:K], exp_top[:, :, 0:K]))
                own.wait_apart()
                for j in range(J):
                    own.mark(V.match_replace(exp_out[:, j, :], exp_rep[:, j, :], exp_in[:, j, :], BIG))
                own.wait()
                own.mark(V.tensor_scalar(sel_all[:, bass.ds(b * J, J), :], exp_out[:, :, 0:E], BIG / 2, None, op0=ALU.is_ge))
                do(V.scalar_tensor_tensor(picked[:, :, :], exp_out[:, :, 0:E], BIG / 2, sc[:, :, :], op0=ALU.is_ge, op1=ALU.mult))
                do(V.tensor_reduce(pick_sum[:, :], picked[:, :, :], AX.X, ALU.add))
                do(V.tensor_scalar(pick_sum[:, :], pick_sum[:, :], 1e-20, None, op0=ALU.add))
                do(V.reciprocal(pick_inv[:, :], pick_sum[:, :]))
                V.scalar_tensor_tensor(rows[par][:, :, D:ROW], picked[:, :, :], wscale[:, 0:1],
                                       pick_inv[:, :].unsqueeze(2).to_broadcast([P, J, E]), op0=ALU.mult,
                                       op1=ALU.mult).then_inc(routed, 1)

            def step(s, h, live):
                now, prev, prev2 = live
                more = now and (not isinstance(s, int) or s + 1 < GROUPS)
                if prev:
                    residual(s - 1, 1 - h, J - 1)
                if more:
                    norm1_stats(s + 1, 1 - h)
                if prev2:
                    route_groups(s - 2, h)
                if prev:
                    norm2_apply(s - 1, 1 - h)
                if now:
                    residual(s, h, 0)
                if prev2:
                    route_masks(s - 2, h)
                if now:
                    residual(s, h, 1)
                if prev2:
                    route_experts(s - 2, h)
                if now:
                    residual(s, h, 2)

            norm1_stats(0, 0)
            zero_beside(1)
            dve.wait_ge(tanh_ready, 1)
            own.mark(V.tensor_scalar(wscale[:, :], tg[:, 1:2], ROUTED_SCALE, None, op0=ALU.mult))
            step(0, 0, (True, False, False))
            step(1, 1, (True, True, False))
            PER_STEP = 40
            start = own.n
            with dve.Fori(*span(2, GROUPS - 2, 2)) as s:
                own.base, own.n = (s - 2) * PER_STEP + start, 0
                for h in range(2):
                    step(s + h, h, (True, True, True))
                assert own.n == 2 * PER_STEP, own.n
            own.base, own.n = 0, start + (GROUPS - 4) * PER_STEP
            step(GROUPS - 2, 0, (True, True, True))
            step(GROUPS - 1, 1, (True, True, True))
            residual(GROUPS - 1, 1, J - 1)
            norm2_apply(GROUPS - 1, 1)
            for b in range(GROUPS - 2, GROUPS):
                route_groups(b, b % 2)
                route_masks(b, b % 2)
                route_experts(b, b % 2)

            dve.wait_ge(consts_ready, 5)
            dve.wait_ge(tables_set, 7)
            dve.wait_ge(prefix_ready, 1)
            V.tensor_copy(tile_picks[:, :], psum[:, 6 * 512:8 * 512].rearrange("p (k q) -> p k q", q=P)[:, :, P - 1]).then_inc(tile_picks_ready, 1)
            dve.wait_ge(bounds_in_psum, 1)
            V.tensor_copy(bounds[:, 1, :], bank[4][:, 0:8])
            V.tensor_tensor(bounds[:, 0, :], bank[4][:, 0:8], tile_picks[:, :], ALU.subtract).then_inc(bounds_copied, 1)
            dve.wait_ge(bounds_copied, 1)
            V.tensor_scalar(marks[:, :, 0], bounds[:, 0, :], 255.0, None, op0=ALU.min).then_inc(slot_bases_ready, 1)
            slotb = slot_row[:, :].unsqueeze(1).to_broadcast([P, 8, P])
            do(V.tensor_tensor(from_lo[:, :, :], slotb, bounds[:, 0, :].unsqueeze(2).to_broadcast([P, 8, P]), ALU.is_ge))
            for k in range(8):
                last = V.scalar_tensor_tensor(onehot[:, k, :], slot_row[:, :], bounds[:, 1, k:k + 1], from_lo[:, k, :],
                                              op0=ALU.is_lt, op1=ALU.mult)
            last.then_inc(onehot_ready, 1)
            dve.wait_ge(slot_marks_in_psum, 1)
            V.tensor_copy(slot_marks[:, :, :].rearrange("p (k q) m -> p k q m", q=4),
                          psum[:, 4 * 512:8 * 512].rearrange("p (q f) -> p q f", q=4)[:, :, 0:E].rearrange("p q (k m) -> p k q m", m=4)
                          ).then_inc(slot_marks_read, 1)
            dve.wait_ge(slot_marks_read, 1)
            base_of, tile_of, filled = slot_marks[:, :, 0], slot_marks[:, :, 1], slot_marks[:, :, 2]
            do(V.tensor_scalar(rank[:, :], base_of, -1.0, slot_col[:, 0:1], op0=ALU.mult, op1=ALU.add))
            V.tensor_scalar(rank_half[:, :], rank[:, :], 0.5, None, op0=ALU.add).then_inc(ranks_ready, 1)
            do(V.tensor_scalar(tok_c[:, :], filled, -1.0, 1.0, op0=ALU.mult, op1=ALU.add))
            do(V.tensor_scalar(tok_c[:, :], tok_c[:, :], spare_col[:, 0:1], None, op0=ALU.mult))
            do(V.scalar_tensor_tensor(tok_b[:, :], tile_of, float(P), tok_c[:, :], op0=ALU.mult, op1=ALU.add))
            for r in range(2):
                for i, q in ((0, 0), (2, 1)):
                    dve.wait_ge(counts_ready, 4 * r + i + 1)
                    for k in range(4):
                        e = 16 * r + 4 * k + q
                        last = V.tensor_scalar(compared[:, e, :], bank[4 + q][:, k * P:k * P + P], rank[:, e:e + 1], 0.0,
                                               op0=ALU.is_le, op1=ALU.add, accum_out=in_tile[:, e:e + 1])
                    last.then_inc(counted_dve, 1)
            dve.wait_ge(counted_dve, 4)
            dve.wait_ge(counted_act, 4)
            act_part = in_tile[:, :].rearrange("p (k q) -> p k q", q=4)[:, :, 2:4]
            do(V.tensor_scalar(act_part, in_sign[:, :].rearrange("p (k q) -> p k q", q=4)[:, :, 2:4], 0.5, P / 2, op0=ALU.mult, op1=ALU.add))
            do(V.tensor_tensor(tok_a[:, :], in_tile[:, :], filled, ALU.mult))
            V.tensor_tensor(tok_id[:, :], tok_a[:, :], tok_b[:, :], ALU.add).then_inc(table_ready, 1)

            def copy_rows_T(e, r):
                dve.wait_ge(xe_in_psum, e + 1)
                wait(dve, he_in_psum, e - 1)
                V.tensor_copy(xeT[r % 2][:, :, :].rearrange("p c s -> p (c s)"), bank[4][:, 0:D]).then_inc(xeT_ready, 1)

            def hidden(e, r):
                dve.wait_ge(he_in_psum, e + 1)
                V.tensor_scalar(relu_e[:, :], bank[5][:, 0:P], 0.0, None, op0=ALU.max).then_inc(he_read, 1)
                dve.wait_ge(he_read, e + 1)
                wait(dve, ye_in_psum, e - 1)
                V.tensor_tensor(h_e[r % 2][:, :], relu_e[:, :], relu_e[:, :], ALU.mult).then_inc(he_ready, 1)

            def weigh(e, r):
                dve.wait_ge(ye_in_psum, e + 1)
                wait(dve, scattered, 16 * (e - 1))
                V.tensor_scalar(y_e[r % 2][:, :], bank[6][:, 0:D], xe[r % RING][:, bass.ds(e + D, 1)], None,
                                op0=ALU.mult).then_inc(ye_ready, 1)

            def slots(n, e0, first, last_):
                for k in range(8):
                    e = e0 + k
                    hidden(e, k)
                    if not (last_ and k == 7):
                        copy_rows_T(e + 1, k + 1)
                    if not (first and k == 0):
                        weigh(e - 1, k + 7)
                    if first and k == 2:
                        split_rows_low(V, n + 1)
                    if k == HC + 1 and has(n + 2):
                        split_rows_low(V, n + 2)

            copy_rows_T(0, 0)
            slots(BEFORE_EXPERTS, 0, True, False)
            with dve.Fori(BEFORE_EXPERTS + 1, BEFORE_EXPERTS + 3) as n:
                slots(n, n * 8 - BEFORE_EXPERTS * 8, False, False)
            slots(BEFORE_EXPERTS + 3, E - 8, False, True)
            weigh(E - 1, 7)


_INS = ("x", "ctx_rows", "ctx_cols", "gates", "gate_w", "bias", "shared_up", "shared_down", "expert_w")


def kernel(x, ctx_2048, g_xattn, g_ffn, L0_ffn_gate_w, L0_ffn_bias_corr, L0_ffn_up_w, L0_ffn_down_w,
           L0_ffn_shared_up_w, L0_ffn_shared_down_w):
    import concourse.bacc as bacc
    from concourse.bass_utils import run_bass_kernel_spmd

    arr = lambda a: np.ascontiguousarray(np.asarray(a))
    x, c = np.asarray(x), np.asarray(ctx_2048)
    B, S, D = x.shape
    E, H, _ = L0_ffn_up_w.shape

    def groups(a):
        return arr(a.reshape(-1, 4, 128, D).transpose(0, 2, 1, 3).reshape(-1, 128, 4 * D))

    def cols(w):
        w = np.asarray(w)
        return arr(w.T.reshape(-1, 128, w.shape[0]).transpose(1, 0, 2).reshape(128, -1))

    ct = arr(c.reshape(-1, 4, 2, S, 2, 128).transpose(0, 5, 1, 4, 2, 3).reshape(-1, 128, 4 * 2 * 128))
    up = np.asarray(L0_ffn_up_w).transpose(0, 2, 1).reshape(E, 2, 128, H).transpose(0, 2, 1, 3).reshape(E, 128, 2 * H)
    down = np.asarray(L0_ffn_down_w).transpose(0, 2, 1)
    arrays = {
        "x": groups(x),
        "ctx_rows": groups(c),
        "ctx_cols": ct,
        "gates": arr(np.broadcast_to(np.stack([np.asarray(g_xattn)[0], np.asarray(g_ffn)[0]]), (128, 2))),
        "gate_w": cols(L0_ffn_gate_w),
        "bias": arr(np.broadcast_to(np.asarray(L0_ffn_bias_corr), (128, E))),
        "shared_up": cols(L0_ffn_shared_up_w),
        "shared_down": cols(L0_ffn_shared_down_w),
        "expert_w": arr(np.concatenate([up, down], axis=2)),
    }
    nc = bacc.Bacc("TRN2", target_bir_lowering=False, num_devices=1)
    aps = [nc.dram_tensor(n, arrays[n].shape, mybir.dt.float32, kind="ExternalInput").ap() for n in _INS]
    out = nc.dram_tensor("out", (B * S + 128, D), mybir.dt.float32, kind="ExternalOutput").ap()
    gated_xattn_moe_block(nc, *aps, out)
    r = run_bass_kernel_spmd(nc, [arrays], core_ids=[0])
    return arr(r.results[0]["out"][:B * S].reshape(B, S, D))
```
